# Optimizing a Trainium2 kernel written in Bass

```python
import numpy as np
import jax
import jax.numpy as jnp

def _softmax(x, axis=-1):
    return jax.nn.softmax(x, axis=axis)

def _gelu(x):
    return jax.nn.gelu(x, approximate=True)

def _silu(x):
    return jax.nn.silu(x)

def _sigmoid(x):
    return jax.nn.sigmoid(x)

def _layernorm(x, axis=-1, eps=1e-05):
    m = jnp.mean(x, axis=axis, keepdims=True)
    v = jnp.var(x, axis=axis, keepdims=True)
    return (x - m) / jnp.sqrt(v + eps)

def _scatter_add(tgt, idx, src, axis=0):
    return tgt.at[idx].add(src)

def _segment_sum(src, seg, n):
    return jax.ops.segment_sum(src, seg, n)
kernel_name = 'mk_xattn_ffn_d1_seqx_r8_a6fa22'

def setup_inputs(seed: int=0):
    np.random.seed(seed)
    _w = jnp.asarray

    def _rec_inputs():
        import jax
        import jax.numpy as jnp
        _rk = jax.random.key(seed)
        x = -0.0002928 + 1 * jax.random.normal(jax.random.fold_in(_rk, 1), (8, 256, 128), jnp.float32)
        _lenS = 256 - jax.random.randint(jax.random.fold_in(_rk, 7), (8,), 0, max(1, 256 // 4) + 1, jnp.int32)
        _lenS2 = 512 - jax.random.randint(jax.random.fold_in(_rk, 8), (8,), 0, max(1, 512 // 4) + 1, jnp.int32)
        _ctx_1024P = jax.random.normal(jax.random.fold_in(_rk, 11), (8, 16, 128), jnp.float32)
        _ctx_1024c = jax.random.dirichlet(jax.random.fold_in(_rk, 511), 0.3 * jnp.ones((16,), jnp.float32), (8, 512))
        _ctx_1024t = jnp.einsum('bsk,bkd->bsd', _ctx_1024c, _ctx_1024P)
        _ctx_1024t = _ctx_1024t * jax.lax.rsqrt(jnp.mean(jnp.square(_ctx_1024t)) + 1e-12) * 0.953939
        ctx_1024 = -1.39393e-06 + 0.999914 * (_ctx_1024t + 0.3 * jax.random.normal(jax.random.fold_in(_rk, 611), (8, 512, 128), jnp.float32))
        _validS = jnp.arange(256)[None, :] < _lenS[:, None]
        _validS2 = jnp.arange(512)[None, :] < _lenS2[:, None]
        _causal = jnp.tril(jnp.ones((256, 256), dtype=bool))
        mask_BxSxS2_bf1 = jnp.ones((8, 256, 512), dtype=bool)
        return (x, ctx_1024, mask_BxSxS2_bf1)
    x, ctx_1024, mask_BxSxS2_bf1 = _rec_inputs()

    def _L0_xattn_setup():
        import jax, jax.numpy as jnp
        import numpy as np
        B, S, D, H = (2, 256, 128, 16)
        DH = D // H

        def _split_heads(x):
            b, s, _ = x.shape
            return x.reshape(b, s, H, DH).transpose(0, 2, 1, 3)
        key = jax.random.key(seed)
        ks = jax.random.split(key, 12)
        scale = 1.0 / np.sqrt(D)
        inp = {'attn_from': jax.random.normal(ks[0], (B, S, D), jnp.float32), 'attn_to': jax.random.normal(ks[1], (B, S, D), jnp.float32), 'value': jax.random.normal(ks[2], (B, S, D), jnp.float32), 'mask': jnp.ones((B, S, S), dtype=bool), 'Wq': jax.random.normal(ks[3], (D, D), jnp.float32) * scale, 'bq': jnp.zeros((D,), jnp.float32), 'Wk': jax.random.normal(ks[4], (D, D), jnp.float32) * scale, 'bk': jnp.zeros((D,), jnp.float32), 'Wv': jax.random.normal(ks[5], (D, D), jnp.float32) * scale, 'bv': jnp.zeros((D,), jnp.float32), 'Wo': jax.random.normal(ks[6], (D, D), jnp.float32) * scale, 'bo': jnp.zeros((D,), jnp.float32)}
        return inp
    _L0_xattn_all = _L0_xattn_setup()
    _L0_xattn_in = {k: v for k, v in _L0_xattn_all.items() if k in ('Wq', 'bq', 'Wk', 'bk', 'Wv', 'bv', 'Wo', 'bo')}
    del _L0_xattn_all

    def _L0_ffn_setup():
        import jax, jax.numpy as jnp
        import numpy as np
        B, S, H, F, E, K = (2, 128, 128, 256, 8, 2)
        key = jax.random.key(seed)
        ks = jax.random.split(key, 5)
        scale_h = 1.0 / np.sqrt(H)
        scale_f = 1.0 / np.sqrt(F)
        return {'inputs': jax.random.normal(ks[0], (B, S, H), dtype=jnp.float32), 'router_w': jax.random.normal(ks[1], (H, E), dtype=jnp.float32) * scale_h, 'w1': jax.random.normal(ks[2], (E, H, F), dtype=jnp.float32) * scale_h, 'w3': jax.random.normal(ks[3], (E, H, F), dtype=jnp.float32) * scale_h, 'w2': jax.random.normal(ks[4], (E, F, H), dtype=jnp.float32) * scale_f}
    _L0_ffn_all = _L0_ffn_setup()
    _L0_ffn_in = {k: v for k, v in _L0_ffn_all.items() if k in ('router_w', 'w1', 'w3', 'w2')}
    del _L0_ffn_all
    return {'x': x, 'ctx_1024': ctx_1024, 'mask_BxSxS2_bf1': mask_BxSxS2_bf1, 'L0_xattn_Wq': _L0_xattn_in['Wq'], 'L0_xattn_bq': _L0_xattn_in['bq'], 'L0_xattn_Wk': _L0_xattn_in['Wk'], 'L0_xattn_bk': _L0_xattn_in['bk'], 'L0_xattn_Wv': _L0_xattn_in['Wv'], 'L0_xattn_bv': _L0_xattn_in['bv'], 'L0_xattn_Wo': _L0_xattn_in['Wo'], 'L0_xattn_bo': _L0_xattn_in['bo'], 'L0_ffn_router_w': _L0_ffn_in['router_w'], 'L0_ffn_w1': _L0_ffn_in['w1'], 'L0_ffn_w3': _L0_ffn_in['w3'], 'L0_ffn_w2': _L0_ffn_in['w2']}

def reference(x, ctx_1024, mask_BxSxS2_bf1, L0_xattn_Wq, L0_xattn_bq, L0_xattn_Wk, L0_xattn_bk, L0_xattn_Wv, L0_xattn_bv, L0_xattn_Wo, L0_xattn_bo, L0_ffn_router_w, L0_ffn_w1, L0_ffn_w3, L0_ffn_w2):
    import jax
    import jax.numpy as jnp

    def _L0_xattn_ref(attn_from, attn_to, value, mask, Wq, bq, Wk, bk, Wv, bv, Wo, bo):
        import jax, jax.numpy as jnp
        import numpy as np
        B, S, D, H = (2, 256, 128, 16)
        DH = D // H

        def _split_heads(x):
            b, s, _ = x.shape
            return x.reshape(b, s, H, DH).transpose(0, 2, 1, 3)
        q = _split_heads(attn_from @ Wq.T + bq)
        k = _split_heads(attn_to @ Wk.T + bk)
        v = _split_heads(value @ Wv.T + bv)
        scores = jnp.einsum('bhqd,bhkd->bhqk', q, k) / jnp.sqrt(jnp.float32(DH))
        scores = jnp.where(mask[:, None, :, :], scores, jnp.float32(-1000000000.0))
        attn = jax.nn.softmax(scores, axis=-1)
        ctx = jnp.einsum('bhqk,bhkd->bhqd', attn, v)
        ctx = ctx.transpose(0, 2, 1, 3).reshape(ctx.shape[0], -1, H * DH)
        return ctx @ Wo.T + bo

    def _L0_ffn_ref(inputs, router_w, w1, w3, w2):
        import jax, jax.numpy as jnp
        import numpy as np
        B, S, H, F, E, K = (2, 128, 128, 256, 8, 2)
        b, s, h = inputs.shape
        x = inputs.reshape(-1, h)
        logits = x @ router_w
        top_vals, top_idx = jax.lax.top_k(logits, K)
        importance = jax.nn.softmax(top_vals.astype(jnp.float32), axis=-1).astype(x.dtype)
        one_hot = top_idx[..., None] == jnp.arange(E)[None, None, :]
        combine = jnp.sum(jnp.where(one_hot, importance[..., None], 0.0), axis=1)
        gate = jax.nn.silu(jnp.einsum('th,ehf->etf', x, w1))
        up = jnp.einsum('th,ehf->etf', x, w3)
        expert_out = jnp.einsum('etf,efh->eth', gate * up, w2)
        out = jnp.einsum('te,eth->th', combine, expert_out)
        return out.reshape(b, s, h)
    x = x + _L0_xattn_ref(_layernorm(x, axis=-1), ctx_1024, ctx_1024, mask_BxSxS2_bf1, L0_xattn_Wq, L0_xattn_bq, L0_xattn_Wk, L0_xattn_bk, L0_xattn_Wv, L0_xattn_bv, L0_xattn_Wo, L0_xattn_bo)
    x = x + _L0_ffn_ref(_layernorm(x, axis=-1), L0_ffn_router_w, L0_ffn_w1, L0_ffn_w3, L0_ffn_w2)
    return x

_drawn_inputs = setup_inputs


def setup_inputs(seed=0):
    import zlib

    import numpy as np

    out = dict(_drawn_inputs(seed))
    spreads = {'L0_xattn_bq': (0.0, 0.1),
     'L0_xattn_bk': (0.0, 0.1),
     'L0_xattn_bv': (0.0, 0.1),
     'L0_xattn_bo': (0.0, 0.1)}
    factors = {}
    for name, (base, spread) in spreads.items():
        noise = np.random.default_rng([zlib.crc32(name.encode()), seed]).standard_normal(out[name].shape)
        drawn = base * np.exp(spread * noise) if base else spread * noise
        out[name] = jnp.asarray(drawn.astype(out[name].dtype))
    for name, factor in factors.items():
        out[name] = (out[name] * factor).astype(out[name].dtype)
    return out
```

```python
from contextlib import ExitStack

import concourse.bass as bass
from concourse import mybir

ALU = mybir.AluOpType
ACT = mybir.ActivationFunctionType
AX = mybir.AxisListType
F32 = mybir.dt.float32
BF16 = mybir.dt.bfloat16
I32 = mybir.dt.int32
U32 = mybir.dt.uint32

P = 128


def xattn_ffn_kernel(nc: bass.Bass, x, ctx_t, mask, wq_t, bq, wk_t, bk, wv_t, bv, wo_t, bo, router_w, w1, w3, w2, out):
    B, S, D = x.shape
    S2 = ctx_t.shape[2]
    H, DH = 16, 8
    E = router_w.shape[1]
    F = w1.shape[2]
    NP = H // 2
    G = 2
    J = NP // G
    QT = S // P
    KC = S2 // P
    NT = B * QT
    FT = F // P
    PART = 3
    ROWS = 2 * 6 * DH
    KROWS = ROWS + 2 * PART
    CH = G * KC * J
    TILES = G * J * 2 * QT
    NST, NS, NPR = 3, 2, 8
    SCALE = float(DH) ** -0.5
    MASKED = 1.0e9 * float(DH) ** 0.5
    EPS = 1e-5
    TC = 4
    TT = NT // TC
    assert CH == 32 and TILES == 32 and ROWS == 96 and QT * P * 2 == 512 and S2 == 512 and E == 8

    x_v = x.rearrange("b (t p) d -> p (b t) d", p=P)
    out_v = out.rearrange("b (t p) d -> p (b t) d", p=P)
    mask_v = mask.rearrange("b (t p) k -> p b t k", p=P)

    with ExitStack() as ctx:
        def sb(name, shape, dt):
            return ctx.enter_context(nc.sbuf_tensor(name, shape, dt))

        def pb(name, shape, dt):
            return ctx.enter_context(nc.psum_tensor(name, shape, dt))

        def sem(name):
            return ctx.enter_context(nc.semaphore(name))

        x_sb = sb("x_sb", [P, NT, D], F32)
        res = sb("res", [P, NT, D], F32)
        ctx_sb = [sb(f"ctx_sb{n}", [P, S2], F32) for n in range(2)]
        mask_sb = sb("mask_sb", [P, B, QT, S2], mask.dtype)
        mbias = sb("mbias", [P, B, QT, S2], BF16)
        msum = sb("msum", [P, 2], F32)
        flag = sb("flag", [1, B], I32)
        wq_sb = sb("wq_sb", [P, D], F32)
        wk_sb = sb("wk_sb", [P, D], F32)
        wv_sb = sb("wv_sb", [P, D], F32)
        wo_sb = sb("wo_sb", [P, D], F32)
        bq_sb = sb("bq_sb", [P, 1], F32)
        bk_sb = sb("bk_sb", [P, 1], F32)
        bv_sb = sb("bv_sb", [P, 1], F32)
        bo_sb = sb("bo_sb", [P, D], F32)
        bvb = sb("bvb", [P, P], F32)
        obias = sb("obias", [P, D], F32)
        rw_sb = sb("rw_sb", [P, E], F32)
        ident = sb("ident", [P, P], F32)
        identb = sb("identb", [P, P], BF16)
        onesf = sb("onesf", [P, P], F32)
        stats = sb("stats", [P, 2, QT, 6], F32)
        mv = sb("mv", [P, 2, QT, 2], F32)
        vareps = sb("vareps", [P, 2, QT], F32)
        minus_half = sb("minus_half", [P, QT], F32)
        rstd = sb("rstd", [P, 2, QT], F32)
        xn = sb("xn", [P, QT, D], F32)
        xnT = sb("xnT", [P, S], F32)
        qf = [sb(f"qf{n}", [P, S], F32) for n in range(2)]
        kf = [sb(f"kf{n}", [P, S2], F32) for n in range(2)]
        qs = sb("qs", [P, PART, S], BF16)
        ks = sb("ks", [P, PART, S2], BF16)
        kst = [sb(f"kst{n}", [P, NP, S2], BF16) for n in range(2)]
        qst = [sb(f"qst{n}", [P, 2, NP, S], BF16) for n in range(2)]
        vx = [sb(f"vx{n}", [P, KC, NP, 2, 16], F32) for n in range(2)]
        nmax = sb("nmax", [P, G, QT * 2, J], F32)
        nrest = sb("nrest", [P, QT * 2, J], F32)
        nsp = sb("nsp", [P, G, QT * 2, PART, J], BF16)
        nrow = sb("nrow", [2 * PART * J, G, S], BF16)
        probs = [sb(f"probs{n}", [P, 2 * S], F32) for n in range(NPR)]
        raw = sb("raw", [P, 2 * S], F32)
        rec = sb("rec", [P, 2, QT, J], F32)
        att = sb("att", [P, QT, 2, NP, DH], F32)
        attT = sb("attT", [P, S], F32)
        xn2 = sb("xn2", [P, QT, D], F32)
        xt2 = sb("xt2", [P, S], F32)
        x2T = sb("x2T", [P, NT * P], F32)
        logits = sb("logits", [P, NT, E], F32)
        w1_sb = sb("w1_sb", [P, E, F], F32)
        w3_sb = sb("w3_sb", [P, E, F], F32)
        w2_sb = sb("w2_sb", [P, E, FT, D], F32)
        top = sb("top", [P, NT, E], F32)
        topi = sb("topi", [P, NT, E], U32)
        topf = sb("topf", [P, NT, 2], F32)
        gap = sb("gap", [P, NT], F32)
        egap = sb("egap", [P, NT], F32)
        gate = sb("gate", [P, 2, NT], F32)
        lane = sb("lane", [P, E], F32)
        lanei = sb("lanei", [P, E], I32)
        comb = sb("comb", [P, NT, E], F32)
        comb2 = sb("comb2", [P, NT, E], F32)
        act_sb = [sb(f"act_sb{n}", [P, TT * P], F32) for n in range(2)]
        hid = [[sb(f"hid{n}{f}", [P, TT * P], F32) for f in range(FT)] for n in range(2)]
        part = [sb(f"part{n}", [P, TT, D], F32) for n in range(2)]

        kd = nc.dram_tensor("k_parts", (2, NP, PART, DH, S2), BF16, kind="Internal").ap()
        qd = nc.dram_tensor("q_parts", (2, NP, PART, DH, S), BF16, kind="Internal").ap()

        ps_t = [pb(f"ps_t{n}", [P, 512], F32) for n in range(NST)]
        ps_s = [pb(f"ps_s{n}", [P, 512], F32) for n in range(NS)]
        ps_pv = pb("ps_pv", [P, 512], F32)
        ps_a = pb("ps_a", [P, 512], F32)
        ps_b = pb("ps_b", [P, 512], F32)

        s_x = sem("s_x"); s_w = sem("s_w"); s_wf = sem("s_wf"); s_ctx = sem("s_ctx"); s_mask = sem("s_mask")
        s_const = sem("s_const"); s_idz = sem("s_idz"); s_ones = sem("s_ones")
        s_bvb = sem("s_bvb"); s_obp = sem("s_obp"); s_ob = sem("s_ob"); s_resx = sem("s_resx")
        s_dve = sem("s_dve"); s_pool = sem("s_pool")
        s_mv1 = sem("s_mv1"); s_rs1 = sem("s_rs1"); s_mv2 = sem("s_mv2"); s_rs2 = sem("s_rs2")
        s_xn = sem("s_xn"); s_xnp = sem("s_xnp"); s_xnT = sem("s_xnT")
        s_qp = sem("s_qp"); s_qf = sem("s_qf"); s_kp = sem("s_kp"); s_kf = sem("s_kf")
        s_vp = sem("s_vp"); s_vx = sem("s_vx")
        s_split = sem("s_split"); s_dram = sem("s_dram"); s_stk = sem("s_stk")
        s_mb = sem("s_mb"); s_mf = sem("s_mf"); s_flag = sem("s_flag")
        s_tile = sem("s_tile"); s_max = sem("s_max"); s_nsp = sem("s_nsp"); s_ntp = sem("s_ntp")
        s_nrow = sem("s_nrow"); s_nst = sem("s_nst")
        s_chunk = sem("s_chunk"); s_exp = sem("s_exp"); s_pv = sem("s_pv"); s_raw = sem("s_raw")
        s_rt = sem("s_rt"); s_att = sem("s_att"); s_atp = sem("s_atp"); s_attT = sem("s_attT")
        s_op = sem("s_op"); s_res = sem("s_res"); s_xn2 = sem("s_xn2"); s_x2p = sem("s_x2p"); s_x2T = sem("s_x2T")
        s_x2c = sem("s_x2c"); s_lp = sem("s_lp"); s_lg = sem("s_lg")
        s_gap = sem("s_gap"); s_egap = sem("s_egap"); s_comb = sem("s_comb")
        s_g = sem("s_g"); s_u = sem("s_u"); s_act = sem("s_act"); s_hid = sem("s_hid"); s_eo = sem("s_eo")
        s_part = sem("s_part"); s_sum = sem("s_sum"); s_out = sem("s_out")

        def wait_first(eng, s, value):
            eng.wait_ge(s, value)
            if not isinstance(value, int):
                eng.wait_ge(s_idz, 6)

        class Chain:

            def __init__(self, s):
                self.s, self.base, self.n = s, 0, 0

            def link(self, eng, ins):
                self.n += 1
                ins.then_inc(self.s, 1)
                wait_first(eng, self.s, self.base + self.n)

        def batches(eng, head, body, chain=None, per_pair=0):
            head()
            for i in range(B):
                body(i, i % 2)

        def early(i, last):
            return not isinstance(i, int) or i < last

        def later(i):
            return not isinstance(i, int) or i > 0

        block = ctx.enter_context(nc.Block())

        @block.sync
        def _(sp):
            def load_ctx(n, par):
                if not isinstance(n, int) or n >= 2:
                    wait_first(sp, s_vp, n - 1)
                sp.dma_start(ctx_sb[par][:, :], ctx_t[n]).then_inc(s_ctx, 16)

            def to_dram(n):
                if not isinstance(n, int) or n > 0:
                    wait_first(sp, s_stk, 24 * 16 * n)
                wait_first(sp, s_split, 6 * n + 6)
                for a in range(PART):
                    sp.dma_start(qd[:, :, a].rearrange("e p d n -> (e p) d n"), qs[:, a, :]).then_inc(s_dram, 16)
                    sp.dma_start(kd[:, :, a].rearrange("e p d n -> (e p) d n"), ks[:, a, :]).then_inc(s_dram, 16)
                wait_first(sp, s_dram, 6 * 16 * (n + 1))

            def stack(n, g, par):
                if not isinstance(n, int) or n >= 2:
                    wait_first(sp, s_chunk, CH * (n - 2) + CH // G * (g + 1))
                ps = slice(J * g, J * g + J)
                for e in range(2):
                    for row, k0, q0, cnt in ((0, 0, 0, 3), (3 * DH, 0, 1, 2), (5 * DH, 0, 2, 1)):
                        rows = slice(6 * DH * e + row, 6 * DH * e + row + cnt * DH)
                        sp.dma_start(kst[par][rows, ps, :],
                                     kd[e, ps, k0:k0 + cnt].rearrange("p a d n -> (a d) p n")).then_inc(s_stk, 16)
                        sp.dma_start(qst[par][rows, e, ps, :],
                                     qd[e, ps, q0:q0 + cnt].rearrange("p a d n -> (a d) p n")).then_inc(s_stk, 16)
                wait_first(sp, s_stk, 12 * 16 * (2 * n + g + 1))

            def max_rows(n, g, par):
                wait_first(sp, s_nrow, 2 * n + g + 1)
                if not isinstance(n, int) or n >= 2:
                    wait_first(sp, s_chunk, CH * (n - 2) + CH // G * (g + 1))
                for e in range(2):
                    for a in range(PART):
                        r = (PART * e + a)
                        sp.dma_start(qst[par][ROWS + r:ROWS + r + 1, e, J * g:J * g + J, :],
                                     nrow[J * r:J * r + J, g, :]).then_inc(s_nst, 16)
                wait_first(sp, s_nst, 6 * 16 * (2 * n + g + 1))

            def head():
                sp.dma_start(x_sb[:, 0:QT, :], x_v[:, 0:QT, :]).then_inc(s_x, 16)
                sp.dma_start(wq_sb[:, :], wq_t).then_inc(s_w, 16)
                sp.dma_start(bq_sb[:, :], bq.rearrange("(p o) -> p o", o=1)).then_inc(s_w, 16)
                load_ctx(0, 0)
                sp.dma_start(wk_sb[:, :], wk_t).then_inc(s_w, 16)
                sp.dma_start(bk_sb[:, :], bk.rearrange("(p o) -> p o", o=1)).then_inc(s_w, 16)
                sp.dma_start(wv_sb[:, :], wv_t).then_inc(s_w, 16)
                sp.dma_start(wo_sb[:, :], wo_t).then_inc(s_w, 16)
                sp.dma_start(bv_sb[:, :], bv.rearrange("(p o) -> p o", o=1)).then_inc(s_w, 16)
                sp.dma_start(bo_sb[:, :], bo.rearrange("(o d) -> o d", o=1).partition_broadcast(P)).then_inc(s_w, 16)
                sp.dma_start(rw_sb[:, :], router_w).then_inc(s_w, 16)
                wait_first(sp, s_x, 16)
                sp.dma_start(x_sb[:, QT:NT, :], x_v[:, QT:NT, :]).then_inc(s_x, 16)
                sp.dma_start(mask_sb[:, :, :, :], mask_v).then_inc(s_mask, 16)
                wait_first(sp, s_ctx, 16)
                load_ctx(1, 1)
                wait_first(sp, s_const, 1)
                to_dram(0)
                stack(0, 0, 0)
                stack(0, 1, 0)
                load_ctx(2, 0)
                to_dram(1)
                stack(1, 0, 1)
                max_rows(0, 0, 0)
                sp.dma_start(w1_sb[:, :, :], w1.rearrange("e h f -> h e f")).then_inc(s_wf, 16)
                sp.dma_start(w3_sb[:, :, :], w3.rearrange("e h f -> h e f")).then_inc(s_wf, 16)
                sp.dma_start(w2_sb[:, :, :, :], w2.rearrange("e (t f) h -> f e t h", f=P)).then_inc(s_wf, 16)

            def body(i, par):
                if early(i, 7):
                    stack(i + 1, 1, 1 - par)
                max_rows(i, 1, par)
                if early(i, 5):
                    wait_first(sp, s_ctx, 16 * (i + 3))
                    load_ctx(i + 3, 1 - par)
                if early(i, 6):
                    to_dram(i + 2)
                    stack(i + 2, 0, par)
                if early(i, 7):
                    max_rows(i + 1, 0, 1 - par)

            batches(sp, head, body)
            with sp.Fori(0, TC) as tc:
                wait_first(sp, s_sum, E * tc + E)
                sp.dma_start(out_v[:, bass.ts(tc, TT), :], res[:, bass.ts(tc, TT), :]).then_inc(s_out, 16)
            wait_first(sp, s_out, 16 * TC)

        @block.gpsimd
        def _(pool):
            chain = Chain(s_pool)

            def rstd_of(which, n, moments, done):
                pool.wait_ge(moments, n + 1)
                pool.tensor_tensor(rstd[:, which, :], vareps[:, which, :], minus_half[:, :], ALU.pow).then_inc(done, 1)

            def split(n, par, between=None):
                if not isinstance(n, int) or n > 0:
                    pool.wait_ge(s_dram, 6 * 16 * n)
                for full, f, o, order in ((s_qf, qf[par], qs, (2, 1, 0)), (s_kf, kf[par], ks, (0, 1, 2))):
                    h, m, l = (o[:, a, :] for a in order)
                    if o is ks and between:
                        between()
                    wait_first(pool, full, n + 1)
                    ins = pool.tensor_copy(h, f[:, :])
                    ins.then_inc(s_split, 1)
                    wait_first(pool, s_split, 6 * n + (1 if o is qs else 4))
                    chain.link(pool, pool.tensor_tensor(f[:, :], f[:, :], h, ALU.subtract))
                    ins = pool.tensor_copy(m, f[:, :])
                    ins.then_inc(s_split, 1)
                    wait_first(pool, s_split, 6 * n + (2 if o is qs else 5))
                    pool.tensor_tensor(l, f[:, :], m, ALU.subtract).then_inc(s_split, 1)

            def head():
                pool.memset(minus_half[:, :], -0.5).then_inc(s_idz, 1)
                pool.memset(ident[:, :], 0.0).then_inc(s_idz, 1)
                pool.memset(identb[:, :], 0.0).then_inc(s_idz, 1)
                pool.wait_ge(s_idz, 3)
                for n, t in enumerate((ident, identb)):
                    pool.affine_select(out=t[:, :], in_=t[:, :], compare_op=ALU.not_equal, fill=1.0, base=0,
                                       pattern=[[-1, P]], channel_multiplier=1).then_inc(s_idz, 1)
                pool.iota(lanei[:, :], pattern=[[1, E]], base=0, channel_multiplier=0).then_inc(s_idz, 1)
                rstd_of(0, 0, s_mv1, s_rs1)
                rstd_of(0, 1, s_mv1, s_rs1)
                split(0, 0)
                rstd_of(0, 2, s_mv1, s_rs1)
                split(1, 1)
                pool.wait_ge(s_ob, 1)
                pool.wait_ge(s_x, 32)
                pool.tensor_tensor(res[:, :, :], x_sb[:, :, :],
                                   obias[:, :].rearrange("p (o d) -> p o d", o=1).to_broadcast([P, NT, D]),
                                   ALU.add).then_inc(s_resx, 1)

            def body(i, par):
                def second():
                    rstd_of(1, i - 1, s_mv2, s_rs2)

                if early(i, 6):
                    split(i + 2, par, second if later(i) else None)
                elif later(i):
                    second()
                if later(i):
                    wait_first(pool, s_x2T, i)
                    pool.tensor_copy(x2T[:, bass.ts(i - 1, S)], xt2[:, :]).then_inc(s_x2c, 1)
                if early(i, 5):
                    rstd_of(0, i + 3, s_mv1, s_rs1)

            batches(pool, head, body, chain, 4)
            rstd_of(1, B - 1, s_mv2, s_rs2)
            pool.wait_ge(s_x2T, B)
            pool.tensor_copy(x2T[:, (B - 1) * S:B * S], xt2[:, :]).then_inc(s_x2c, 1)
            for tc in range(TC):
                for e in range(E):
                    wait_first(pool, s_part, E * tc + e + 1)
                    if e or tc:
                        wait_first(pool, s_sum, E * tc + e)
                    r = res[:, tc * TT:(tc + 1) * TT, :]
                    pool.tensor_tensor(r, r, part[e % 2][:, :, :], ALU.add).then_inc(s_sum, 1)

        @block.tensor
        def _(pe):
            def xn_turn(n):
                pe.wait_ge(s_xn, n + 1)
                for t in range(QT):
                    ins = pe.transpose(ps_b[:, t * P:(t + 1) * P], xn[:, t, :], ident[:, :])
                ins.then_inc(s_xnp, 1)

            def q_proj(n):
                pe.wait_ge(s_xnT, n + 1)
                pe.matmul(ps_b[:, 0:S], wq_sb[:, :], xnT[:, :], start=True, stop=True).then_inc(s_qp, 1)

            def k_proj(n, par):
                pe.wait_ge(s_qf, n + 1)
                pe.wait_ge(s_ctx, 16 * (n + 1))
                pe.matmul(ps_b[:, :], wk_sb[:, :], ctx_sb[par][:, :], start=True, stop=True).then_inc(s_kp, 1)

            def v_proj(n, par):
                for c in range(KC):
                    ins = pe.matmul(ps_b[:, c * D:(c + 1) * D], ctx_sb[par][:, c * P:(c + 1) * P], wv_sb[:, :],
                                    start=True, stop=True)
                ins.then_inc(s_vp, 1)

            def mask_sum(n, par):
                pe.wait_ge(s_mb, n + 1)
                pe.matmul(ps_b[0:1, 0:1], msum[:, par:par + 1], onesf[:, 0:1], start=True, stop=True).then_inc(s_mf, 1)

            def turn_max(n, g, bank):
                pe.wait_ge(s_nsp, 2 * n + g + 1)
                for t in range(QT):
                    ins = pe.transpose(bank[:, :].bitcast(BF16)[0:2 * PART * J, t * P:(t + 1) * P],
                                       nsp[:, g, 2 * t:2 * t + 2].rearrange("p e a j -> p (e a j)"), identb[:, :])
                ins.then_inc(s_ntp, 1)

            def tile(n, s, par, masked):
                g, j, e, t = s // 16, s // 4 % 4, s // 2 % 2, s % 2
                p = J * g + j
                if s % 16 == 0:
                    pe.wait_ge(s_stk, 12 * 16 * (2 * n + g + 1))
                if not isinstance(n, int) or n > 0 or s >= NS:
                    pe.wait_ge(s_max, TILES * n + s - NS + 1)
                ins = pe.matmul(ps_s[s % NS][:, :], qst[par][0:ROWS, e, p, t * P:(t + 1) * P], kst[par][0:ROWS, p, :],
                                start=True, stop=not masked)
                if masked:
                    ins = pe.matmul(ps_s[s % NS][:, :], identb[:, :], mbias[:, n, t, :], start=False, stop=True)
                ins.then_inc(s_tile, 1)

            def chunk(n, c, par, masked):
                g, kc, j = c // 16, c // 4 % 4, c % 4
                p = J * g + j
                if c % 16 == 0:
                    pe.wait_ge(s_nst, 6 * 16 * (2 * n + g + 1))
                if not isinstance(n, int) or n > 0 or c >= NST:
                    pe.wait_ge(s_exp, CH * n + c - (1 if c < 2 else 2))
                bank = ps_t[c % NST]
                ks_ = slice(kc * P, (kc + 1) * P)
                ins = pe.matmul(bank[:, :].rearrange("k (e q) -> k e q", e=2), kst[par][0:KROWS, p, ks_],
                                qst[par][0:KROWS, :, p, :], start=True, stop=not masked)
                if masked:
                    for t in range(QT):
                        ins = pe.matmul(
                            bank[:, :].rearrange("k (e t q) -> k t e q", e=2, t=QT)[:, t],
                            mbias[:, n, t, ks_],
                            identb[:, :].rearrange("p (o q) -> p o q", o=1).to_broadcast([P, 2, P]),
                            start=False, stop=(t == QT - 1))
                ins.then_inc(s_chunk, 1)

            def values(n, k, par):
                g, kc = k // 4, k % 4
                pe.wait_ge(s_exp, CH * n + 4 * k + 4)
                if k == 0:
                    pe.wait_ge(s_vx, n + 1)
                if kc == 0 and (not isinstance(n, int) or n > 0 or g > 0):
                    pe.wait_ge(s_raw, 2 * n + g)
                for j in range(J):
                    ins = pe.matmul(ps_pv[32 * j:32 * j + 32, :],
                                    vx[par][:, kc, J * g + j].rearrange("k e d -> k (e d)"),
                                    probs[(4 * k + j) % NPR][:, :], start=(kc == 0), stop=(kc == KC - 1))
                ins.then_inc(s_pv, 1)

            def turn_raw(n, g):
                pe.wait_ge(s_raw, 2 * n + g + 1)
                for a in range(2 * QT):
                    ins = pe.transpose(ps_a[:, a * P:(a + 1) * P], raw[:, a * P:(a + 1) * P], ident[:, :])
                ins.then_inc(s_rt, 1)

            def turn_att(n):
                pe.wait_ge(s_att, 2 * n + 2)
                for t in range(QT):
                    ins = pe.transpose(ps_a[:, t * P:(t + 1) * P], att[:, t].rearrange("q e p d -> q (e p d)"),
                                       ident[:, :])
                ins.then_inc(s_atp, 1)

            def out_proj(n):
                pe.wait_ge(s_attT, n + 1)
                for t in range(QT):
                    ins = pe.matmul(ps_a[:, t * D:(t + 1) * D], attT[:, t * P:(t + 1) * P], wo_sb[:, :],
                                    start=True, stop=True)
                ins.then_inc(s_op, 1)

            def turn_xn2(n):
                pe.wait_ge(s_xn2, n + 1)
                for t in range(QT):
                    ins = pe.transpose(ps_a[:, t * P:(t + 1) * P], xn2[:, t, :], ident[:, :])
                ins.then_inc(s_x2p, 1)

            def router(n):
                pe.wait_ge(s_x2T, n + 1)
                for t in range(QT):
                    ins = pe.matmul(ps_a[:, t * E:(t + 1) * E], xt2[:, t * P:(t + 1) * P], rw_sb[:, :],
                                    start=True, stop=True)
                ins.then_inc(s_lp, 1)

            def steps(i, par, masked):
                for s in range(CH):
                    chunk(i, s, par, masked)
                    if early(i, 7):
                        tile(i + 1, s, 1 - par, masked)
                    if s % 4 == 1 and s > 1:
                        values(i, s // 4 - 1, par)
                    if s == 1 and later(i):
                        values(i - 1, 7, 1 - par)
                    if s == 2:
                        if later(i):
                            pe.wait_ge(s_att, 2 * i - 1)
                        turn_max(i, 1, ps_a)
                    if s == 6:
                        if later(i):
                            pe.wait_ge(s_nrow, 2 * i + 2)
                            turn_raw(i - 1, 1)
                        if early(i, 6):
                            pe.wait_ge(s_kf, i + 3)
                            pe.wait_ge(s_nrow, 2 * i + 1)
                            mask_sum(i + 2, par)
                    if s == 9 and later(i):
                        turn_att(i - 1)
                    if s == 10 and early(i, 7):
                        if early(i, 6):
                            pe.wait_ge(s_flag, i + 3)
                        pe.wait_ge(s_nrow, 2 * i + 1)
                        v_proj(i + 1, 1 - par)
                    if s == 11 and later(i):
                        out_proj(i - 1)
                    if s == 15 and later(i):
                        pe.wait_ge(s_res, i)
                        turn_xn2(i - 1)
                    if s == 17 and later(i):
                        router(i - 1)
                    if s == 19 and early(i, 7):
                        pe.wait_ge(s_vx, i + 2)
                        turn_max(i + 1, 0, ps_b)
                    if s == 22:
                        if later(i):
                            pe.wait_ge(s_lg, i)
                        pe.wait_ge(s_nrow, 2 * i + 2)
                        turn_raw(i, 0)
                    if s == 22 and early(i, 5):
                        pe.wait_ge(s_nrow, 2 * i + 3)
                        xn_turn(i + 3)
                    if s == 25 and early(i, 5):
                        q_proj(i + 3)
                    if s == 28 and early(i, 5):
                        k_proj(i + 3, 1 - par)

            def either(cond, emit):
                with pe.If(cond > 0):
                    emit(True)
                with pe.Else():
                    emit(False)

            def head():
                pe.wait_ge(s_idz, 6)
                pe.wait_ge(s_ones, 1)
                pe.wait_ge(s_w, 16 * 9)
                xn_turn(0)
                q_proj(0)
                k_proj(0, 0)
                pe.wait_ge(s_kf, 1)
                xn_turn(1)
                q_proj(1)
                k_proj(1, 1)
                pe.wait_ge(s_bvb, 1)
                pe.matmul(ps_a[:, 0:D], bvb[:, :], wo_sb[:, :], start=True, stop=True).then_inc(s_obp, 1)
                pe.wait_ge(s_kf, 2)
                mask_sum(0, 0)
                pe.wait_ge(s_flag, 1)
                mask_sum(1, 1)
                pe.wait_ge(s_flag, 2)
                v_proj(0, 0)
                either(pe.value_load(flag[0:1, 0:1], min_val=0, max_val=1),
                       lambda masked: [tile(0, s, 0, masked) for s in range(TILES)])
                pe.wait_ge(s_vx, 1)
                turn_max(0, 0, ps_b)
                pe.wait_ge(s_nrow, 1)
                xn_turn(2)
                q_proj(2)
                k_proj(2, 0)
                pe.wait_ge(s_ob, 1)

            def body(i, par):
                if early(i, 7):
                    wait_first(pe, s_flag, i + 2)
                    two = pe.value_load(flag[0:1, bass.ds(i, 1)], min_val=0, max_val=1) + \
                        pe.value_load(flag[0:1, bass.ds(i + 1, 1)], min_val=0, max_val=1)
                else:
                    two = pe.value_load(flag[0:1, i:i + 1], min_val=0, max_val=1)
                either(two, lambda masked: steps(i, par, masked))

            batches(pe, head, body)
            values(B - 1, 7, (B - 1) % 2)
            pe.wait_ge(s_att, 2 * B - 1)
            turn_raw(B - 1, 1)
            turn_att(B - 1)
            out_proj(B - 1)
            pe.wait_ge(s_res, B)
            turn_xn2(B - 1)
            router(B - 1)

            gu = [(ps_t[0], ps_t[1]), (ps_s[0], ps_s[1])]
            eo = [ps_b, ps_pv]
            pe.wait_ge(s_wf, 48)
            pe.wait_ge(s_x2c, B)
            pe.wait_ge(s_exp, CH * B)
            pe.wait_ge(s_max, TILES * B)

            def up(tc, e):
                for f in range(FT):
                    u = FT * e + f
                    rhs = x2T[:, bass.ts(tc, TT * P)]
                    if tc_later or u >= 2:
                        pe.wait_ge(s_act, 2 * E * tc + u - 1)
                    pe.matmul(gu[f][0][:, :], w1_sb[:, e, f * P:(f + 1) * P], rhs, start=True, stop=True).then_inc(s_g, 1)
                    if tc_later or u >= 2:
                        pe.wait_ge(s_hid, 2 * E * tc + u - 1)
                    pe.matmul(gu[f][1][:, :], w3_sb[:, e, f * P:(f + 1) * P], rhs, start=True, stop=True).then_inc(s_u, 1)

            def down(tc, e):
                pe.wait_ge(s_hid, 2 * E * tc + 2 * e + 2)
                if tc_later or e >= 2:
                    pe.wait_ge(s_part, E * tc + e - 1)
                for t in range(TT):
                    for f in range(FT):
                        ins = pe.matmul(eo[e % 2][:, t * D:(t + 1) * D], hid[e % 2][f][:, t * P:(t + 1) * P],
                                        w2_sb[:, e, f, :], start=(f == 0), stop=(f == FT - 1))
                ins.then_inc(s_eo, 1)

            def chunk_of_tokens(tc):
                up(tc, 0)
                for e in range(E):
                    if e + 1 < E:
                        up(tc, e + 1)
                    down(tc, e)

            tc_later = False
            chunk_of_tokens(0)
            tc_later = True
            with pe.Fori(1, TC) as tc:
                chunk_of_tokens(tc)

        @block.scalar
        def _(act):
            def mask_bias(n, par):
                if isinstance(n, int) and n == 0:
                    act.wait_ge(s_mask, 16)
                if not isinstance(n, int) or n >= 2:
                    act.wait_ge(s_mf, n - 1)
                act.activation(mbias[:, n], mask_sb[:, n], ACT.Copy, bias=-MASKED, scale=MASKED,
                               accum_out=msum[:, par:par + 1]).then_inc(s_mb, 1)

            def xnT_copy(n):
                act.wait_ge(s_xnp, n + 1)
                act.activation(xnT[:, :], ps_b[:, 0:S], ACT.Copy).then_inc(s_xnT, 1)

            def q_copy(n, par):
                act.wait_ge(s_qp, n + 1)
                if not isinstance(n, int) or n >= 2:
                    act.wait_ge(s_split, 6 * (n - 2) + 3)
                act.activation(qf[par][:, :], ps_b[:, 0:S], ACT.Identity, bias=bq_sb[:, :]).then_inc(s_qf, 1)

            def k_copy(n, par):
                act.wait_ge(s_kp, n + 1)
                if not isinstance(n, int) or n >= 2:
                    act.wait_ge(s_split, 6 * (n - 2) + 6)
                act.activation(kf[par][:, :], ps_b[:, :], ACT.Identity, bias=bk_sb[:, :]).then_inc(s_kf, 1)

            def v_copy(n, par):
                act.wait_ge(s_vp, n + 1)
                if not isinstance(n, int) or n >= 2:
                    act.wait_ge(s_pv, 8 * (n - 1))
                act.activation(vx[par][:, :, :, :, 0:DH].rearrange("k c p e d -> k (c p e) d"),
                               ps_b[:, :].rearrange("k (h d) -> k h d", d=DH), ACT.Copy).then_inc(s_vx, 1)

            def nrow_copy(n, g, bank):
                act.wait_ge(s_ntp, 2 * n + g + 1)
                if not isinstance(n, int) or n > 0:
                    act.wait_ge(s_nst, 6 * 16 * (2 * n + g - 1))
                act.activation(nrow[:, g, :], bank[:, :].bitcast(BF16)[0:2 * PART * J, 0:S],
                               ACT.Copy).then_inc(s_nrow, 1)

            def exp(n, c):
                act.wait_ge(s_chunk, CH * n + c + 1)
                k = (CH * n + c - NPR) // 4 if isinstance(n, int) else 8 * n + (c - NPR) // 4
                if not isinstance(n, int) or k >= 0:
                    act.wait_ge(s_pv, k + 1)
                act.activation(probs[c % NPR][:, :], ps_t[c % NST][:, :], ACT.Exp, scale=SCALE).then_inc(s_exp, 1)

            def raw_copy(n, g):
                act.wait_ge(s_pv, 8 * n + 4 * g + 4)
                if not isinstance(n, int) or n > 0 or g > 0:
                    act.wait_ge(s_rt, 2 * n + g)
                act.activation(raw[:, :], ps_pv[:, :], ACT.Copy).then_inc(s_raw, 1)

            def attT_copy(n):
                act.wait_ge(s_atp, n + 1)
                act.activation(attT[:, :], ps_a[:, 0:S], ACT.Copy).then_inc(s_attT, 1)

            def xt2_copy(n):
                act.wait_ge(s_x2p, n + 1)
                if not isinstance(n, int) or n > 0:
                    act.wait_ge(s_x2c, n)
                    act.wait_ge(s_lp, n)
                act.activation(xt2[:, :], ps_a[:, 0:S], ACT.Copy).then_inc(s_x2T, 1)

            def head():
                act.wait_ge(s_w, 16 * 9)
                xnT_copy(0)
                q_copy(0, 0)
                k_copy(0, 0)
                xnT_copy(1)
                q_copy(1, 1)
                k_copy(1, 1)
                mask_bias(0, 0)
                mask_bias(1, 1)
                act.wait_ge(s_const, 1)
                v_copy(0, 0)
                nrow_copy(0, 0, ps_b)
                xnT_copy(2)
                q_copy(2, 0)
                k_copy(2, 0)

            def body(i, par):
                for s in range(CH):
                    exp(i, s)
                    if s == 2:
                        if later(i):
                            raw_copy(i - 1, 1)
                        nrow_copy(i, 1, ps_a)
                    if s == 4 and early(i, 6):
                        mask_bias(i + 2, par)
                    if s == 9 and later(i):
                        attT_copy(i - 1)
                    if s == 10 and early(i, 7):
                        v_copy(i + 1, 1 - par)
                    if s == 15 and later(i):
                        xt2_copy(i - 1)
                    if s == 18:
                        raw_copy(i, 0)
                    if s == 19 and early(i, 7):
                        nrow_copy(i + 1, 0, ps_b)
                    if s == 22 and early(i, 5):
                        xnT_copy(i + 3)
                    if s == 25 and early(i, 5):
                        q_copy(i + 3, 1 - par)
                    if s == 28 and early(i, 5):
                        k_copy(i + 3, 1 - par)

            batches(act, head, body)
            raw_copy(B - 1, 1)
            attT_copy(B - 1)
            xt2_copy(B - 1)
            act.wait_ge(s_gap, 1)
            act.activation(egap[:, :], gap[:, :], ACT.Exp).then_inc(s_egap, 1)

            def silu(tc, u, first):
                act.wait_ge(s_g, 2 * E * tc + u + 1)
                if not first:
                    act.wait_ge(s_hid, 2 * E * tc + u - 1)
                act.activation(act_sb[u % 2][:, :], (ps_t, ps_s)[u % 2][0][:, :], ACT.Silu).then_inc(s_act, 1)

            for u in range(FT * E):
                silu(0, u, u < 2)
            with act.Fori(1, TC) as tc:
                for u in range(FT * E):
                    silu(tc, u, False)

        @block.vector
        def _(dve):
            chain = Chain(s_dve)

            def moments(which, src, done):
                for t in range(QT):
                    ins = dve.bn_stats(stats[:, which, t, :], src[t])
                chain.link(dve, ins)
                for t in range(QT):
                    ins = dve.bn_aggr(mv[:, which, t, :], stats[:, which, t, :])
                chain.link(dve, ins)
                dve.tensor_scalar(vareps[:, which, :], mv[:, which, :, 1], EPS, None, ALU.add).then_inc(done, 1)

            def scaled(which, src, dst, done):
                for t in range(QT):
                    ins = dve.tensor_scalar(dst[:, t, :], src[t], mv[:, which, t, 0:1], rstd[:, which, t:t + 1],
                                            ALU.subtract, ALU.mult)
                ins.then_inc(done, 1)

            def norm1_moments(n):
                moments(0, [x_sb[:, 2 * n + t, :] for t in range(QT)], s_mv1)

            def norm1(n):
                dve.wait_ge(s_rs1, n + 1)
                if not isinstance(n, int) or n > 0:
                    dve.wait_ge(s_xnp, n)
                scaled(0, [x_sb[:, 2 * n + t, :] for t in range(QT)], xn, s_xn)

            def norm2(n):
                dve.wait_ge(s_rs2, n + 1)
                if not isinstance(n, int) or n > 0:
                    dve.wait_ge(s_x2p, n)
                scaled(1, [res[:, 2 * n + t, :] for t in range(QT)], xn2, s_xn2)

            def row_max(n, s):
                g, j, e, t = s // 16, s // 4 % 4, s // 2 % 2, s % 2
                dve.wait_ge(s_tile, TILES * n + s + 1)
                dve.tensor_reduce(nmax[:, g, 2 * t + e, j:j + 1], ps_s[s % NS][:, :], AX.X, ALU.max,
                                  negate=True).then_inc(s_max, 1)

            def max_parts(n, g):
                dve.wait_ge(s_max, TILES * n + 16 * (g + 1))
                if not isinstance(n, int) or n > 0:
                    dve.wait_ge(s_ntp, 2 * n + g - 1)
                src = nmax[:, g]
                h, m, l = (nsp[:, g, :, a, :] for a in range(PART))
                chain.link(dve, dve.tensor_copy(h, src))
                chain.link(dve, dve.tensor_tensor(nrest[:, :, :], src, h, ALU.subtract))
                chain.link(dve, dve.tensor_copy(m, nrest[:, :, :]))
                chain.link(dve, dve.tensor_tensor(nrest[:, :, :], nrest[:, :, :], m, ALU.subtract))
                dve.tensor_copy(l, nrest[:, :, :]).then_inc(s_nsp, 1)

            def mask_flag(n):
                dve.wait_ge(s_mf, n + 1)
                dve.tensor_scalar(flag[0:1, bass.ds(n, 1)], ps_b[0:1, 0:1], 0.0, None, ALU.is_lt).then_inc(s_flag, 1)

            def normalise(n, g):
                dve.wait_ge(s_rt, 2 * n + g + 1)
                if g == 0 and (not isinstance(n, int) or n > 0):
                    dve.wait_ge(s_atp, n)
                for e in range(2):
                    v = ps_a[:, 2 * P * e:2 * P * (e + 1)].rearrange("q (t j r) -> q t j r", t=QT, j=J)
                    ins = dve.reciprocal(rec[:, e], v[:, :, :, 16 * e + DH])
                chain.link(dve, ins)
                for e in range(2):
                    v = ps_a[:, 2 * P * e:2 * P * (e + 1)].rearrange("q (t j r) -> q t j r", t=QT, j=J)
                    ins = dve.tensor_tensor(
                        att[:, :, e, J * g:J * g + J, :], v[:, :, :, 16 * e:16 * e + DH],
                        rec[:, e].rearrange("q t (j o) -> q t j o", o=1).to_broadcast([P, QT, J, DH]), ALU.mult)
                ins.then_inc(s_att, 1)

            def residual(n):
                dve.wait_ge(s_op, n + 1)
                if isinstance(n, int) and n == 0:
                    dve.wait_ge(s_resx, 1)
                r = res[:, bass.ts(n, QT), :]
                dve.tensor_tensor(r, ps_a[:, 0:QT * D].rearrange("q (t d) -> q t d", t=QT), r, ALU.add).then_inc(s_res, 1)
                wait_first(dve, s_res, n + 1)
                moments(1, [res[:, 2 * n + t, :] for t in range(QT)], s_mv2)

            def logits_copy(n):
                dve.wait_ge(s_lp, n + 1)
                dve.tensor_copy(logits[:, bass.ts(n, QT), :],
                                ps_a[:, 0:QT * E].rearrange("q (t e) -> q t e", t=QT)).then_inc(s_lg, 1)

            def head():
                dve.memset(onesf[:, :], 1.0).then_inc(s_ones, 1)
                dve.wait_ge(s_x, 16)
                norm1_moments(0)
                norm1(0)
                dve.memset(qst[0][:, :, :, :], 0.0)
                dve.memset(kst[0][96:128, :, :], 1.0)
                dve.memset(qst[1][:, :, :, :], 0.0)
                dve.memset(kst[1][96:128, :, :], 1.0)
                dve.memset(vx[0][:, :, :, :, :], 1.0)
                dve.memset(vx[1][:, :, :, :, :], 1.0).then_inc(s_const, 1)
                dve.wait_ge(s_x, 32)
                norm1_moments(1)
                norm1(1)
                dve.wait_ge(s_ones, 1)
                dve.wait_ge(s_w, 16 * 9)
                dve.tensor_scalar(bvb[:, :], onesf[:, :], bv_sb[:, 0:1], None, ALU.mult).then_inc(s_bvb, 1)
                dve.wait_ge(s_obp, 1)
                dve.tensor_tensor(obias[:, :], ps_a[:, 0:D], bo_sb[:, :], ALU.add).then_inc(s_ob, 1)
                mask_flag(0)
                mask_flag(1)
                norm1_moments(2)
                norm1(2)
                for s in range(TILES):
                    row_max(0, s)
                    if s == 15:
                        max_parts(0, 0)
                max_parts(0, 1)

            def body(i, par):
                for s in range(CH):
                    if early(i, 7):
                        row_max(i + 1, s)
                    if s == 6:
                        if later(i):
                            normalise(i - 1, 1)
                        if early(i, 6):
                            mask_flag(i + 2)
                    if s == 11 and later(i):
                        residual(i - 1)
                    if s == 13 and later(i):
                        norm2(i - 1)
                    if s == 15 and early(i, 7):
                        max_parts(i + 1, 0)
                    if s == 17:
                        if later(i):
                            logits_copy(i - 1)
                        if early(i, 5):
                            norm1_moments(i + 3)
                    if s == 20 and early(i, 5):
                        norm1(i + 3)
                    if s == 22:
                        normalise(i, 0)
                if early(i, 7):
                    max_parts(i + 1, 1)

            batches(dve, head, body, chain, 2 * (1 + 2 + 4 + 2 + 1 + 4))
            normalise(B - 1, 1)
            residual(B - 1)
            norm2(B - 1)
            logits_copy(B - 1)
            dve.wait_ge(s_lg, B)
            dve.wait_ge(s_idz, 6)
            for t in range(NT):
                ins = dve.max(top[:, t, :], logits[:, t, :])
            chain.link(dve, ins)
            dve.tensor_tensor(gap[:, :], top[:, :, 1], top[:, :, 0], ALU.subtract).then_inc(s_gap, 1)
            for t in range(NT):
                ins = dve.max_index(topi[:, t, :], top[:, t, :], logits[:, t, :])
            chain.link(dve, ins)
            dve.tensor_copy(topf[:, :, :], topi[:, :, 0:2])
            chain.link(dve, dve.tensor_copy(lane[:, :], lanei[:, :]))
            dve.wait_ge(s_egap, 1)
            chain.link(dve, dve.tensor_scalar(gate[:, 1, :], egap[:, :], 1.0, None, ALU.add))
            chain.link(dve, dve.reciprocal(gate[:, 0, :], gate[:, 1, :]))
            chain.link(dve, dve.tensor_tensor(gate[:, 1, :], egap[:, :], gate[:, 0, :], ALU.mult))

            def over(ap):
                return ap.rearrange("q (t o) -> q t o", o=1).to_broadcast([P, NT, E])

            for k, c in ((0, comb), (1, comb2)):
                chain.link(dve, dve.tensor_tensor(c[:, :, :],
                                                  lane[:, :].rearrange("q (o e) -> q o e", o=1).to_broadcast([P, NT, E]),
                                                  over(topf[:, :, k]), ALU.is_equal))
                chain.link(dve, dve.tensor_tensor(c[:, :, :], c[:, :, :], over(gate[:, k, :]), ALU.mult))
            chain.link(dve, dve.tensor_tensor(comb[:, :, :], comb[:, :, :], comb2[:, :, :], ALU.add))

            def gated(tc, u, first):
                e, f = u // FT, u % FT
                dve.wait_ge(s_act, 2 * E * tc + u + 1)
                dve.wait_ge(s_u, 2 * E * tc + u + 1)
                if not first:
                    dve.wait_ge(s_eo, E * tc + e - 1)
                dve.tensor_tensor(hid[e % 2][f][:, :], (ps_t, ps_s)[u % 2][1][:, :], act_sb[u % 2][:, :],
                                  ALU.mult).then_inc(s_hid, 1)

            def weigh(tc, e, first):
                dve.wait_ge(s_eo, E * tc + e + 1)
                if not first:
                    dve.wait_ge(s_sum, E * tc + e - 1)
                c = comb[:, bass.ts(tc, TT), e:e + 1].to_broadcast([P, TT, D])
                dve.tensor_tensor(part[e % 2][:, :, :], (ps_b, ps_pv)[e % 2][:, :].rearrange("q (t d) -> q t d", t=TT), c,
                                  ALU.mult).then_inc(s_part, 1)

            def chunk_of_tokens(tc, first):
                for e in range(E):
                    for f in range(FT):
                        gated(tc, FT * e + f, first and e < 2)
                    if e:
                        weigh(tc, e - 1, first and e - 1 < 2)
                weigh(tc, E - 1, False)

            chunk_of_tokens(0, True)
            with dve.Fori(1, TC) as tc:
                chunk_of_tokens(tc, False)


def kernel(x, ctx_1024, mask_BxSxS2_bf1, L0_xattn_Wq, L0_xattn_bq, L0_xattn_Wk, L0_xattn_bk, L0_xattn_Wv, L0_xattn_bv,
           L0_xattn_Wo, L0_xattn_bo, L0_ffn_router_w, L0_ffn_w1, L0_ffn_w3, L0_ffn_w2):
    import numpy as np
    import concourse.bacc as bacc
    from concourse.bass_utils import run_bass_kernel_spmd

    def turned(w):
        return np.ascontiguousarray(np.asarray(w).T)

    wv = turned(L0_xattn_Wv)
    d = wv.shape[0]
    arrays = {
        "x": np.ascontiguousarray(x),
        "ctx_t": np.ascontiguousarray(np.asarray(ctx_1024).transpose(0, 2, 1)),
        "mask": np.ascontiguousarray(mask_BxSxS2_bf1).view(np.uint8),
        "wq_t": turned(L0_xattn_Wq), "bq": np.ascontiguousarray(L0_xattn_bq),
        "wk_t": turned(L0_xattn_Wk), "bk": np.ascontiguousarray(L0_xattn_bk),
        "wv_t": np.ascontiguousarray(wv.reshape(d, 2, 8, 8).transpose(0, 2, 1, 3).reshape(d, d)),
        "bv": np.ascontiguousarray(L0_xattn_bv),
        "wo_t": turned(L0_xattn_Wo), "bo": np.ascontiguousarray(L0_xattn_bo),
        "router_w": np.ascontiguousarray(L0_ffn_router_w),
        "w1": np.ascontiguousarray(L0_ffn_w1), "w3": np.ascontiguousarray(L0_ffn_w3),
        "w2": np.ascontiguousarray(L0_ffn_w2),
    }
    nc = bacc.Bacc("TRN2", target_bir_lowering=False, num_devices=1)
    ins = {n: nc.dram_tensor(f"in_{n}", a.shape, mybir.dt.from_np(a.dtype), kind="ExternalInput").ap()
           for n, a in arrays.items()}
    out = nc.dram_tensor("out_x", arrays["x"].shape, F32, kind="ExternalOutput").ap()
    xattn_ffn_kernel(nc, **ins, out=out)
    r = run_bass_kernel_spmd(nc, [{f"in_{n}": a for n, a in arrays.items()}], core_ids=[0])
    return r.results[0]["out_x"]
```

```python
from contextlib import ExitStack

import concourse.bass as bass
from concourse import mybir

ALU = mybir.AluOpType
ACT = mybir.ActivationFunctionType
AX = mybir.AxisListType
F32 = mybir.dt.float32
F32R = mybir.dt.float32r
BF16 = mybir.dt.bfloat16
I32 = mybir.dt.int32
U32 = mybir.dt.uint32

P = 128


def xattn_ffn_kernel(nc: bass.Bass, x, ctx_t, mask, wq_t, bq, wk_t, bk, wv_t, bv, wo_t, bo, router_w, w13, w2, out):
    B, S, D = x.shape
    S2 = ctx_t.shape[2]
    H, DH = 16, 8
    E = router_w.shape[1]
    WP, _, WN = w13.shape
    F = WN // 2
    NP = H // 2
    G = 2
    J = NP // G
    QT = S // P
    KC = S2 // P
    NT = B * QT
    FT = F // P
    PART = 3
    ROWS = 2 * 6 * DH
    KROWS = ROWS + 2 * PART
    CH = G * KC * J
    TILES = G * J * 2 * QT
    SHIFT = 14
    NST, NS, NPR = 3, 2, 8
    SCALE = float(DH) ** -0.5
    MASKED = 1.0e9 * float(DH) ** 0.5
    EPS = 1e-5
    TC = 4
    TT = NT // TC
    ROUTED = slice(0, NT - QT), slice(NT - QT, NT)
    LEAD = CH - 8
    assert CH == 32 and TILES == 32 and ROWS == 96 and QT * P * 2 == 512 and S2 == 512 and E == 8

    x_v = x.rearrange("b (t p) d -> p (b t) d", p=P)
    out_v = out.rearrange("b (t p) d -> p (b t) d", p=P)
    mask_v = mask.rearrange("b (t p) k -> p b t k", p=P)

    with ExitStack() as ctx:
        def sb(name, shape, dt):
            return ctx.enter_context(nc.sbuf_tensor(name, shape, dt))

        def pb(name, shape, dt):
            return ctx.enter_context(nc.psum_tensor(name, shape, dt))

        def sem(name):
            return ctx.enter_context(nc.semaphore(name))

        x_sb = sb("x_sb", [P, NT, D], F32)
        res = sb("res", [P, NT, D], F32)
        ctx_sb = [sb(f"ctx_sb{n}", [P, S2], F32) for n in range(2)]
        mask_sb = sb("mask_sb", [P, 2, QT, S2], mask.dtype)
        mbias = sb("mbias", [P, B, QT, S2], BF16)
        msum = sb("msum", [P, 2], F32)
        flag = sb("flag", [1, B], I32)
        wq_sb = sb("wq_sb", [P, D], F32)
        wk_sb = sb("wk_sb", [P, D], F32)
        wv_sb = sb("wv_sb", [P, D], F32)
        wo_sb = sb("wo_sb", [P, D], F32)
        bq_sb = sb("bq_sb", [P, 1], F32)
        bk_sb = sb("bk_sb", [P, 1], F32)
        bv_sb = sb("bv_sb", [P, 1], F32)
        bo_sb = sb("bo_sb", [P, D], F32)
        bvb = sb("bvb", [P, P], F32)
        obias = sb("obias", [P, D], F32)
        rw_sb = sb("rw_sb", [P, E], F32)
        ident = sb("ident", [P, P], F32)
        identb = sb("identb", [P, P], BF16)
        onesf = sb("onesf", [P, P], F32)
        stats = sb("stats", [P, 2, QT, 6], F32)
        mv = sb("mv", [P, 2, QT, 2], F32)
        vareps = sb("vareps", [P, 2, QT], F32)
        minus_half = sb("minus_half", [P, QT], F32)
        rstd = sb("rstd", [P, 2, QT], F32)
        xn = sb("xn", [P, QT, D], F32)
        xnT = sb("xnT", [P, S], F32)
        qf = [sb(f"qf{n}", [P, S], F32) for n in range(2)]
        kf = [sb(f"kf{n}", [P, S2], F32) for n in range(2)]
        qs = sb("qs", [P, PART, S], BF16)
        ks = sb("ks", [P, PART, S2], BF16)
        kst = [sb(f"kst{n}", [P, NP, S2], BF16) for n in range(2)]
        qst = [sb(f"qst{n}", [P, 2, NP, S], BF16) for n in range(2)]
        vx = [sb(f"vx{n}", [P, KC, NP, 2, 16], F32) for n in range(2)]
        nmax = sb("nmax", [P, G, QT * 2, J], F32)
        nrest = sb("nrest", [P, QT * 2, J], F32)
        nsp = sb("nsp", [P, G, QT * 2, PART, J], BF16)
        nrow = sb("nrow", [2 * PART * J, G, S], BF16)
        probs = [sb(f"probs{n}", [P, 2 * S], F32) for n in range(NPR)]
        raw = sb("raw", [P, 2 * S], F32)
        rec = sb("rec", [P, 2, QT, J], F32)
        att = sb("att", [P, QT, 2, NP, DH], F32)
        attT = sb("attT", [P, S], F32)
        xn2 = sb("xn2", [P, QT, D], F32)
        xt2 = sb("xt2", [P, S], F32)
        x2h = sb("x2h", [P, NT * P], F32R)
        x2l = sb("x2l", [P, NT * P], F32R)
        logits = sb("logits", [P, NT, E], F32)
        wst = [sb(f"wst{n}", [P, WN], F32) for n in range(2)]
        wh = sb("wh", [P, WP, WN], F32R)
        wl = sb("wl", [P, WP, WN], F32R)
        w2_sb = sb("w2_sb", [P, E, FT, D], F32)
        top = sb("top", [P, NT, E], F32)
        topi = sb("topi", [P, NT, E], U32)
        topf = sb("topf", [P, NT, 2], F32)
        gap = sb("gap", [P, NT], F32)
        egap = sb("egap", [P, NT], F32)
        gate = sb("gate", [P, 2, NT], F32)
        lane = sb("lane", [P, E], F32)
        lanei = sb("lanei", [P, E], I32)
        comb = sb("comb", [P, NT, E], F32)
        comb2 = top
        act_sb, hid = probs[0:2], (probs[2:4], probs[6:8])
        part = probs[4:6]

        TERMS = ((0, 0, 3), (3, 0, 2), (5, 0, 1)), ((0, 0, 3), (3, 1, 2), (5, 2, 1))
        kd = nc.dram_tensor("k_stack", (6, 2 * DH, NP, S2), BF16, kind="Internal").ap()
        qd = nc.dram_tensor("q_stack", (2, 6, 2, DH, NP, S), BF16, kind="Internal").ap()

        ps_t = [pb(f"ps_t{n}", [P, 512], F32) for n in range(NST)]
        ps_s = [pb(f"ps_s{n}", [P, 512], F32) for n in range(NS)]
        ps_pv = pb("ps_pv", [P, 512], F32)
        ps_a = pb("ps_a", [P, 512], F32)
        ps_b = pb("ps_b", [P, 512], F32)

        s_x = sem("s_x"); s_w = sem("s_w"); s_vo = sem("s_vo"); s_wf = [sem("s_wf0"), sem("s_wf1")]; s_wh = sem("s_wh"); s_wl = sem("s_wl"); s_w2 = sem("s_w2"); s_zero = sem("s_zero"); s_ctx = sem("s_ctx"); s_mask = sem("s_mask")
        s_const = sem("s_const"); s_idz = sem("s_idz"); s_ones = sem("s_ones")
        s_bvb = sem("s_bvb"); s_obp = sem("s_obp"); s_ob = sem("s_ob"); s_resx = sem("s_resx")
        s_dve = sem("s_dve"); s_pool = sem("s_pool")
        s_mv1 = sem("s_mv1"); s_rs1 = sem("s_rs1"); s_mv2 = sem("s_mv2"); s_rs2 = sem("s_rs2")
        s_xn = sem("s_xn"); s_xnp = sem("s_xnp"); s_xnT = sem("s_xnT")
        s_qp = sem("s_qp"); s_qf = sem("s_qf"); s_kp = sem("s_kp"); s_kf = sem("s_kf")
        s_vp = sem("s_vp"); s_vx = sem("s_vx")
        s_split = sem("s_split"); s_dram = sem("s_dram"); s_stk = [sem("s_stk0"), sem("s_stk1")]
        s_mb = sem("s_mb"); s_mf = sem("s_mf"); s_flag = sem("s_flag")
        s_tile = sem("s_tile"); s_max = sem("s_max"); s_nsp = sem("s_nsp"); s_ntp = sem("s_ntp")
        s_nrow = sem("s_nrow"); s_nst = [sem("s_nst0"), sem("s_nst1")]
        s_chunk = sem("s_chunk"); s_exp = sem("s_exp"); s_pv = sem("s_pv"); s_raw = sem("s_raw")
        s_rt = sem("s_rt"); s_att = sem("s_att"); s_atp = sem("s_atp"); s_attT = sem("s_attT")
        s_op = sem("s_op"); s_res = sem("s_res"); s_xn2 = sem("s_xn2"); s_x2p = sem("s_x2p"); s_x2T = sem("s_x2T")
        s_x2h = sem("s_x2h"); s_x2c = sem("s_x2c"); s_lp = sem("s_lp"); s_lg = sem("s_lg")
        s_gap = sem("s_gap"); s_egap = sem("s_egap"); s_comb = sem("s_comb")
        s_g = sem("s_g"); s_u = sem("s_u"); s_act = sem("s_act"); s_hid = sem("s_hid"); s_eo = sem("s_eo")
        s_part = sem("s_part"); s_sum = sem("s_sum"); s_out = sem("s_out")

        def wait_first(eng, s, value):
            eng.wait_ge(s, value)
            if not isinstance(value, int):
                eng.wait_ge(s_idz, 6)

        class Chain:

            def __init__(self, s):
                self.s, self.base, self.n = s, 0, 0

            def mark(self, ins):
                self.n += 1
                ins.then_inc(self.s, 1)

            def settle(self, eng):
                wait_first(eng, self.s, self.base + self.n)

            def link(self, eng, ins):
                self.mark(ins)
                self.settle(eng)

        def batches(eng, head, body, chain=None, per_pair=0):
            head()
            for i in range(B):
                body(i, i % 2)

        def bank_of(c):
            return (c if c < SHIFT else c + 1) % NST, 2 if c in (SHIFT, SHIFT + 1) else 5 if c == SHIFT + 2 else 3

        def early(i, last):
            return not isinstance(i, int) or i < last

        def in_loop(i):
            return not isinstance(i, int) or 1 <= i < 5

        def later(i):
            return not isinstance(i, int) or i > 0

        block = ctx.enter_context(nc.Block())

        @block.sync
        def _(sp):
            def load_ctx(n, par):
                if not isinstance(n, int) or n >= 2:
                    wait_first(sp, s_vp, n - 1)
                sp.dma_start(ctx_sb[par][:, :], ctx_t[n]).then_inc(s_ctx, 16)

            def load_mask(n, par):
                if not isinstance(n, int) or n >= 2:
                    sp.wait_ge(s_mb, n - 1)
                sp.dma_start(mask_sb[:, par], mask_v[:, n]).then_inc(s_mask, 16)

            def to_dram(n):
                if not isinstance(n, int) or n > 0:
                    for g in range(G):
                        sp.wait_ge(s_stk[g], 2 * 16 * n)
                sp.wait_ge(s_split, 6 * n + 3)
                for t, a, cnt in TERMS[1]:
                    for e in range(2):
                        sp.dma_start(qd[e, t:t + cnt, e].rearrange("t d p n -> (d p) t n"),
                                     qs[64 * e:64 * e + 64, a:a + cnt, :]).then_inc(s_dram, 16)
                sp.wait_ge(s_split, 6 * n + 6)
                for t, a, cnt in TERMS[0]:
                    sp.dma_start(kd[t:t + cnt].rearrange("t r p n -> (r p) t n"), ks[:, a:a + cnt, :]).then_inc(s_dram, 16)
                sp.wait_ge(s_dram, 16 * (9 * n + 11))

            def stack(n, g, par):
                if not isinstance(n, int) or n >= 2:
                    sp.wait_ge(s_chunk, CH * (n - 2) + CH // G * (g + 1))
                ps = slice(J * g, J * g + J)
                sp.dma_start(kst[par][0:ROWS, ps, :],
                             kd[:, :, ps].rearrange("t r p n -> (t r) p n")).then_inc(s_stk[g], 16)
                sp.dma_start(qst[par][0:ROWS, :, ps, :].rearrange("r e p n -> r e (p n)"),
                             qd[:, :, :, :, ps].rearrange("s t e d p n -> (t e d) s (p n)")).then_inc(s_stk[g], 16)

            def max_rows(n, g, par):
                wait_first(sp, s_nrow, 2 * n + g + 1)
                if not isinstance(n, int) or n >= 2:
                    wait_first(sp, s_chunk, CH * (n - 2) + CH // G * (g + 1))
                for e in range(2):
                    r = PART * e
                    sp.dma_start(qst[par][ROWS + r:ROWS + r + PART, e, J * g:J * g + J, :],
                                 nrow[J * r:J * (r + PART), g, :]).then_inc(s_nst[g], 16)

            def head():
                sp.dma_start(x_sb[:, 0:QT, :], x_v[:, 0:QT, :]).then_inc(s_x, 16)
                sp.dma_start(wq_sb[:, :], wq_t).then_inc(s_w, 16)
                sp.dma_start(bq_sb[:, :], bq.rearrange("(p o) -> p o", o=1)).then_inc(s_w, 16)
                load_ctx(0, 0)
                sp.dma_start(wk_sb[:, :], wk_t).then_inc(s_w, 16)
                sp.dma_start(bk_sb[:, :], bk.rearrange("(p o) -> p o", o=1)).then_inc(s_w, 16)
                sp.wait_ge(s_zero, 1)
                for e in range(2):
                    sp.dma_start(qd[e, :, 1 - e].rearrange("t d p n -> t d (p n)"),
                                 qst[1][0:6 * DH, 0, :, :].rearrange("r p n -> r (p n)")).then_inc(s_dram, 16)
                load_mask(0, 0)
                sp.wait_ge(s_x, 16)
                sp.dma_start(x_sb[:, QT:NT, :], x_v[:, QT:NT, :]).then_inc(s_x, 16)
                for dst, src in ((wv_sb, wv_t), (wo_sb, wo_t), (rw_sb, router_w)):
                    sp.dma_start(dst[:, :], src).then_inc(s_vo, 16)
                sp.dma_start(bv_sb[:, :], bv.rearrange("(p o) -> p o", o=1)).then_inc(s_vo, 16)
                sp.dma_start(bo_sb[:, :], bo.rearrange("(o d) -> o d", o=1).partition_broadcast(P)).then_inc(s_vo, 16)
                sp.wait_ge(s_mask, 16)
                load_mask(1, 1)
                sp.wait_ge(s_ctx, 16)
                load_ctx(1, 1)
                sp.wait_ge(s_dram, 32)
                to_dram(0)
                stack(0, 0, 0)
                stack(0, 1, 0)
                load_ctx(2, 0)
                to_dram(1)
                max_rows(0, 0, 0)
                stack(1, 0, 1)
                sp.wait_ge(s_mask, 32)
                load_mask(2, 0)

            def weights(i):
                for h in range(2):
                    if not isinstance(i, int) or i > 1:
                        sp.wait_ge(s_wl, 2 * (i - 1))
                    sp.dma_start(wst[h][:, :], w13[2 * (i - 1) + h]).then_inc(s_wf[h], 16)

            def body(i, par):
                if early(i, 7):
                    stack(i + 1, 1, 1 - par)
                if in_loop(i):
                    weights(i)
                max_rows(i, 1, par)
                if early(i, 5):
                    sp.wait_ge(s_ctx, 16 * (i + 3))
                    load_ctx(i + 3, 1 - par)
                    sp.wait_ge(s_mask, 16 * (i + 3))
                    load_mask(i + 3, 1 - par)
                if early(i, 6):
                    to_dram(i + 2)
                if early(i, 7):
                    max_rows(i + 1, 0, 1 - par)
                if early(i, 6):
                    stack(i + 2, 0, par)

            batches(sp, head, body)
            sp.dma_start(w2_sb[:, :, :, :], w2.rearrange("e (f p) d -> p e f d", p=P)).then_inc(s_w2, 16)
            with sp.Fori(0, TC) as tc:
                wait_first(sp, s_sum, E * tc + E)
                sp.dma_start(out_v[:, bass.ts(tc, TT), :], res[:, bass.ts(tc, TT), :]).then_inc(s_out, 16)
            wait_first(sp, s_out, 16 * TC)

        @block.gpsimd
        def _(pool):
            chain = Chain(s_pool)

            def rstd_of(which, n, moments, done):
                pool.wait_ge(moments, n + 1)
                pool.tensor_tensor(rstd[:, which, :], vareps[:, which, :], minus_half[:, :], ALU.pow).then_inc(done, 1)

            def split(n, par, between=None):
                pool.wait_ge(s_dram, 16 * (9 * n + 2))
                for full, f, o, order in ((s_qf, qf[par], qs, (2, 1, 0)), (s_kf, kf[par], ks, (0, 1, 2))):
                    h, m, l = (o[:, a, :] for a in order)
                    done = 6 * n + (0 if o is qs else 3)
                    wait_first(pool, full, n + 1)
                    pool.tensor_copy(h, f[:, :]).then_inc(s_split, 1)
                    wait_first(pool, s_split, done + 1)
                    chain.link(pool, pool.tensor_tensor(f[:, :], f[:, :], h, ALU.subtract))
                    if o is ks and between:
                        between()
                    pool.tensor_copy(m, f[:, :]).then_inc(s_split, 1)
                    wait_first(pool, s_split, done + 2)
                    pool.tensor_tensor(l, f[:, :], m, ALU.subtract).then_inc(s_split, 1)

            def head():
                pool.memset(minus_half[:, :], -0.5).then_inc(s_idz, 1)
                pool.memset(ident[:, :], 0.0).then_inc(s_idz, 1)
                pool.memset(identb[:, :], 0.0).then_inc(s_idz, 1)
                pool.wait_ge(s_idz, 3)
                for n, t in enumerate((ident, identb)):
                    pool.affine_select(out=t[:, :], in_=t[:, :], compare_op=ALU.not_equal, fill=1.0, base=0,
                                       pattern=[[-1, P]], channel_multiplier=1).then_inc(s_idz, 1)
                pool.iota(lanei[:, :], pattern=[[1, E]], base=0, channel_multiplier=0).then_inc(s_idz, 1)
                rstd_of(0, 0, s_mv1, s_rs1)
                pool.wait_ge(s_rs1, 1)
                for n in range(2):
                    pool.memset(kst[n][ROWS:P, :, :], 1.0).then_inc(s_const, 1)
                pool.wait_ge(s_const, 2)
                rstd_of(0, 1, s_mv1, s_rs1)
                rstd_of(0, 2, s_mv1, s_rs1)
                split(1, 1)
                pool.wait_ge(s_ob, 1)
                pool.wait_ge(s_x, 32)
                pool.tensor_tensor(res[:, :, :], x_sb[:, :, :],
                                   obias[:, :].rearrange("p (o d) -> p o d", o=1).to_broadcast([P, NT, D]),
                                   ALU.add).then_inc(s_resx, 1)

            def x2_parts(n):
                wait_first(pool, s_x2T, n + 1)
                pool.tensor_copy(x2h[:, bass.ts(n, S)], xt2[:, :]).then_inc(s_x2h, 1)
                wait_first(pool, s_x2h, n + 1)
                pool.tensor_tensor(x2l[:, bass.ts(n, S)], xt2[:, :], x2h[:, bass.ts(n, S)], ALU.subtract).then_inc(s_x2c, 1)

            def body(i, par):
                def second():
                    rstd_of(1, i - 1, s_mv2, s_rs2)

                if early(i, 6):
                    split(i + 2, par, second if later(i) else None)
                elif later(i):
                    second()
                if early(i, 5):
                    rstd_of(0, i + 3, s_mv1, s_rs1)
                if later(i):
                    x2_parts(i - 1)
                if in_loop(i):
                    for h in range(2):
                        m = 2 * (i - 1) + h
                        wait_first(pool, s_wh, m + 1)
                        pool.tensor_tensor(wl[:, bass.ds(m, 1), :].rearrange("p o n -> p (o n)"), wst[h][:, :],
                                           wh[:, bass.ds(m, 1), :].rearrange("p o n -> p (o n)"),
                                           ALU.subtract).then_inc(s_wl, 1)

            batches(pool, head, body, chain, 4)
            for tc in range(TC):
                for e in range(E):
                    if tc == 0 and e == 2:
                        rstd_of(1, B - 1, s_mv2, s_rs2)
                    if tc == 0 and e == 4:
                        x2_parts(B - 1)
                    pool.wait_ge(s_part, E * tc + e + 1)
                    if e or tc:
                        pool.wait_ge(s_sum, E * tc + e)
                    r = res[:, tc * TT:(tc + 1) * TT, :]
                    pool.tensor_tensor(r, r, part[e % 2][:, :].rearrange("q (t d) -> q t d", t=TT), ALU.add).then_inc(s_sum, 1)

        @block.tensor
        def _(pe):
            def xn_turn(n):
                pe.wait_ge(s_xn, n + 1)
                for t in range(QT):
                    ins = pe.transpose(ps_b[:, t * P:(t + 1) * P], xn[:, t, :], ident[:, :])
                ins.then_inc(s_xnp, 1)

            def q_proj(n):
                pe.wait_ge(s_xnT, n + 1)
                pe.matmul(ps_b[:, 0:S], wq_sb[:, :], xnT[:, :], start=True, stop=True).then_inc(s_qp, 1)

            def k_proj(n, par):
                pe.wait_ge(s_qf, n + 1)
                pe.wait_ge(s_ctx, 16 * (n + 1))
                pe.matmul(ps_b[:, :], wk_sb[:, :], ctx_sb[par][:, :], start=True, stop=True).then_inc(s_kp, 1)

            def v_proj(n, par):
                for c in range(KC):
                    ins = pe.matmul(ps_b[:, c * D:(c + 1) * D], ctx_sb[par][:, c * P:(c + 1) * P], wv_sb[:, :],
                                    start=True, stop=True)
                ins.then_inc(s_vp, 1)

            def mask_sum(n, par):
                pe.wait_ge(s_mb, n + 1)
                both = not isinstance(n, int) or n > 0
                if both:
                    pe.matmul(ps_b[0:1, 0:1], msum[:, 1 - par:2 - par], onesf[:, 0:1], start=True, stop=False)
                pe.matmul(ps_b[0:1, 0:1], msum[:, par:par + 1], onesf[:, 0:1], start=not both, stop=True).then_inc(s_mf, 1)

            def turn_max(n, g, bank):
                pe.wait_ge(s_nsp, 2 * n + g + 1)
                for t in range(QT):
                    ins = pe.transpose(bank[:, :].bitcast(BF16)[0:2 * PART * J, t * P:(t + 1) * P],
                                       nsp[:, g, 2 * t:2 * t + 2].rearrange("p e a j -> p (e a j)"), identb[:, :])
                ins.then_inc(s_ntp, 1)

            def tile(n, s, par, masked):
                g, j, e, t = s // 16, s // 4 % 4, s // 2 % 2, s % 2
                p = J * g + j
                if s % 16 == 0:
                    pe.wait_ge(s_stk[g], 2 * 16 * (n + 1))
                if not isinstance(n, int) or n > 0 or s >= NS:
                    pe.wait_ge(s_max, TILES * n + s - NS + 1)
                ins = pe.matmul(ps_s[s % NS][:, :], qst[par][0:ROWS, e, p, t * P:(t + 1) * P], kst[par][0:ROWS, p, :],
                                start=True, stop=not masked)
                if masked:
                    ins = pe.matmul(ps_s[s % NS][:, :], identb[:, :], mbias[:, n, t, :], start=False, stop=True)
                ins.then_inc(s_tile, 1)

            def chunk(n, c, par, masked):
                g, kc, j = c // 16, c // 4 % 4, c % 4
                p = J * g + j
                if c % 16 == 0:
                    pe.wait_ge(s_nst[g], 2 * 16 * (n + 1))
                if not isinstance(n, int) or n > 0 or c >= NST:
                    pe.wait_ge(s_exp, CH * n + c - bank_of(c)[1] + 1)
                bank = ps_t[bank_of(c)[0]]
                ks_ = slice(kc * P, (kc + 1) * P)
                ins = pe.matmul(bank[:, :].rearrange("k (e q) -> k e q", e=2), kst[par][0:KROWS, p, ks_],
                                qst[par][0:KROWS, :, p, :], start=True, stop=not masked)
                if masked:
                    for t in range(QT):
                        ins = pe.matmul(
                            bank[:, :].rearrange("k (e t q) -> k t e q", e=2, t=QT)[:, t],
                            mbias[:, n, t, ks_],
                            identb[:, :].rearrange("p (o q) -> p o q", o=1).to_broadcast([P, 2, P]),
                            start=False, stop=(t == QT - 1))
                ins.then_inc(s_chunk, 1)

            def values(n, k, par):
                g, kc = k // 4, k % 4
                pe.wait_ge(s_exp, CH * n + 4 * k + 4)
                if k == 0:
                    pe.wait_ge(s_vx, n + 1)
                if kc == 0 and (not isinstance(n, int) or n > 0 or g > 0):
                    pe.wait_ge(s_raw, 2 * n + g)
                for j in range(J):
                    ins = pe.matmul(ps_pv[32 * j:32 * j + 32, :],
                                    vx[par][:, kc, J * g + j].rearrange("k e d -> k (e d)"),
                                    probs[(4 * k + j) % NPR][:, :], start=(kc == 0), stop=(kc == KC - 1))
                ins.then_inc(s_pv, 1)

            def turn_raw(n, g):
                pe.wait_ge(s_raw, 2 * n + g + 1)
                for a in range(2 * QT):
                    ins = pe.transpose(ps_a[:, a * P:(a + 1) * P], raw[:, a * P:(a + 1) * P], ident[:, :])
                ins.then_inc(s_rt, 1)

            def turn_att(n):
                pe.wait_ge(s_att, 2 * n + 2)
                for t in range(QT):
                    ins = pe.transpose(ps_a[:, t * P:(t + 1) * P], att[:, t].rearrange("q e p d -> q (e p d)"),
                                       ident[:, :])
                ins.then_inc(s_atp, 1)

            def out_proj(n):
                pe.wait_ge(s_attT, n + 1)
                for t in range(QT):
                    ins = pe.matmul(ps_a[:, t * D:(t + 1) * D], attT[:, t * P:(t + 1) * P], wo_sb[:, :],
                                    start=True, stop=True)
                ins.then_inc(s_op, 1)

            def turn_xn2(n):
                pe.wait_ge(s_xn2, n + 1)
                for t in range(QT):
                    ins = pe.transpose(ps_a[:, t * P:(t + 1) * P], xn2[:, t, :], ident[:, :])
                ins.then_inc(s_x2p, 1)

            def router(n):
                pe.wait_ge(s_x2T, n + 1)
                for t in range(QT):
                    ins = pe.matmul(ps_a[:, t * E:(t + 1) * E], xt2[:, t * P:(t + 1) * P], rw_sb[:, :],
                                    start=True, stop=True)
                ins.then_inc(s_lp, 1)

            def tile_at(i, par, s, masked):
                if s + LEAD < TILES:
                    tile(i, s + LEAD, par, masked)
                elif early(i, 7):
                    tile(i + 1, s + LEAD - TILES, 1 - par, masked)

            def steps(i, par, masked):
                for s in range(CH):
                    chunk(i, s, par, masked)
                    tile_at(i, par, s, masked)
                    if s % 4 == 1 and s > 1:
                        values(i, s // 4 - 1, par)
                    if s == 1 and later(i):
                        values(i - 1, 7, 1 - par)
                    if s == 2 and early(i, 6):
                        pe.wait_ge(s_kf, i + 3)
                        mask_sum(i + 2, par)
                    if s == 4 and later(i):
                        pe.wait_ge(s_nrow, 2 * i + 1)
                        turn_raw(i - 1, 1)
                    if s == 6 and later(i):
                        turn_att(i - 1)
                    if s == 8 and later(i):
                        out_proj(i - 1)
                    if s == 10:
                        if early(i, 6):
                            pe.wait_ge(s_flag, i + 3)
                        turn_max(i, 1, ps_b)
                    if s == 16 and later(i):
                        pe.wait_ge(s_res, i)
                        turn_xn2(i - 1)
                    if s == 13 and early(i, 7):
                        pe.wait_ge(s_nrow, 2 * i + 2)
                        v_proj(i + 1, 1 - par)
                    if s == 19 and later(i):
                        router(i - 1)
                    if s == 21 and early(i, 5):
                        pe.wait_ge(s_vx, i + 2)
                        xn_turn(i + 3)
                    if s == 23 and early(i, 5):
                        q_proj(i + 3)
                    if s == 22:
                        if later(i):
                            pe.wait_ge(s_lg, i)
                        else:
                            pe.wait_ge(s_nrow, 1)
                        turn_raw(i, 0)
                    if s == 26 and early(i, 5):
                        k_proj(i + 3, 1 - par)
                    if s == 25 and early(i, 7):
                        pe.wait_ge(s_att, 2 * i + 1)
                        turn_max(i + 1, 0, ps_a)

            def either(cond, emit):
                with pe.If(cond > 0):
                    emit(True)
                with pe.Else():
                    emit(False)

            def head():
                pe.wait_ge(s_idz, 6)
                xn_turn(0)
                pe.wait_ge(s_w, 16 * 4)
                q_proj(0)
                k_proj(0, 0)
                pe.wait_ge(s_kf, 1)
                mask_sum(0, 0)
                pe.wait_ge(s_flag, 1)
                mask_sum(1, 1)
                pe.wait_ge(s_vo, 16 * 5)
                pe.wait_ge(s_flag, 2)
                v_proj(0, 0)
                pe.wait_ge(s_bvb, 1)
                pe.matmul(ps_a[:, 0:D], bvb[:, :], wo_sb[:, :], start=True, stop=True).then_inc(s_obp, 1)
                pe.wait_ge(s_vx, 1)
                xn_turn(1)
                q_proj(1)
                pe.wait_ge(s_const, 2)

                def first_tiles(masked):
                    for s in range(LEAD):
                        tile(0, s, 0, masked)
                        if s == 1:
                            k_proj(1, 1)
                        if s == 8:
                            pe.wait_ge(s_kf, 2)
                            xn_turn(2)
                        if s == 11:
                            q_proj(2)
                        if s == 14:
                            k_proj(2, 0)
                        if s == 18:
                            pe.wait_ge(s_ob, 1)
                            turn_max(0, 0, ps_a)

                either(pe.value_load(flag[0:1, 0:1]), first_tiles)

            def body(i, par):
                last = i + 1 if early(i, 7) else i
                either(pe.value_load(flag[0:1, bass.ds(last, 1)]), lambda masked: steps(i, par, masked))

            batches(pe, head, body)
            values(B - 1, 7, (B - 1) % 2)
            gu = [(ps_t[0], ps_t[1]), (ps_s[0], ps_s[1])]
            eo = [ps_b, ps_pv]
            pe.wait_ge(s_wl, WP)
            pe.wait_ge(s_w2, 16)
            pe.wait_ge(s_x2c, B - 1)
            pe.wait_ge(s_exp, CH * B)
            pe.wait_ge(s_max, TILES * B)
            WE = WP // 2

            def up(tc, e, first):
                xh, xl = x2h[:, bass.ts(tc, TT * P)], x2l[:, bass.ts(tc, TT * P)]
                for f in range(FT):
                    u = FT * e + f
                    col = (e % 2) * F + f * P
                    if not first or u >= 2:
                        pe.wait_ge(s_act, FT * E * tc + u - 1)
                    for k, (w, y) in enumerate(((wh, xh), (wl, xh), (wh, xl))):
                        ins = pe.matmul(gu[f][0][:, :], w[:, e // 2, col:col + P], y, start=(k == 0), stop=(k == 2))
                    ins.then_inc(s_g, 1)
                    if not first or u >= 2:
                        pe.wait_ge(s_hid, FT * E * tc + u - 1)
                    for k, (w, y) in enumerate(((wh, xh), (wl, xh), (wh, xl))):
                        ins = pe.matmul(gu[f][1][:, :], w[:, WE + e // 2, col:col + P], y, start=(k == 0), stop=(k == 2))
                    ins.then_inc(s_u, 1)

            def down(tc, e, first):
                pe.wait_ge(s_hid, FT * (E * tc + e + 1))
                if not first or e >= 2:
                    pe.wait_ge(s_part, E * tc + e - 1)
                elif e == 1:
                    pe.wait_ge(s_raw, 2 * B)
                for t in range(TT):
                    for f in range(FT):
                        ins = pe.matmul(eo[e % 2][:, t * D:(t + 1) * D], hid[e % 2][f][:, t * P:(t + 1) * P],
                                        w2_sb[:, e, f, :], start=(f == 0), stop=(f == FT - 1))
                ins.then_inc(s_eo, 1)

            def last_tail(e):
                if e == 0:
                    pe.wait_ge(s_att, 2 * B - 1)
                    turn_raw(B - 1, 1)
                elif e == 1:
                    turn_att(B - 1)
                elif e == 2:
                    out_proj(B - 1)
                elif e == 4:
                    pe.wait_ge(s_res, B)
                    turn_xn2(B - 1)
                elif e == 5:
                    router(B - 1)

            def chunk_of_tokens(tc, first):
                up(tc, 0, first)
                for e in range(E):
                    if e + 1 < E:
                        up(tc, e + 1, first)
                    if first:
                        last_tail(e)
                    down(tc, e, first)

            chunk_of_tokens(0, True)
            pe.wait_ge(s_x2c, B)
            with pe.Fori(1, TC) as tc:
                chunk_of_tokens(tc, False)

        @block.scalar
        def _(act):
            def mask_bias(n, par):
                act.wait_ge(s_mask, 16 * (n + 1))
                if not isinstance(n, int) or n >= 2:
                    act.wait_ge(s_mf, n)
                act.activation(mbias[:, n], mask_sb[:, par], ACT.Copy, bias=-MASKED, scale=MASKED,
                               accum_out=msum[:, par:par + 1]).then_inc(s_mb, 1)

            def xnT_copy(n):
                act.wait_ge(s_xnp, n + 1)
                act.activation(xnT[:, :], ps_b[:, 0:S], ACT.Copy).then_inc(s_xnT, 1)

            def q_copy(n, par):
                act.wait_ge(s_qp, n + 1)
                if not isinstance(n, int) or n >= 2:
                    act.wait_ge(s_split, 6 * (n - 2) + 3)
                act.activation(qf[par][:, :], ps_b[:, 0:S], ACT.Identity, bias=bq_sb[:, :]).then_inc(s_qf, 1)

            def k_copy(n, par):
                act.wait_ge(s_kp, n + 1)
                if not isinstance(n, int) or n >= 2:
                    act.wait_ge(s_split, 6 * (n - 2) + 6)
                act.activation(kf[par][:, :], ps_b[:, :], ACT.Identity, bias=bk_sb[:, :]).then_inc(s_kf, 1)

            def v_copy(n, par):
                act.wait_ge(s_vp, n + 1)
                if not isinstance(n, int) or n >= 2:
                    act.wait_ge(s_pv, 8 * (n - 1))
                act.activation(vx[par][:, :, :, :, 0:DH].rearrange("k c p e d -> k (c p e) d"),
                               ps_b[:, :].rearrange("k (h d) -> k h d", d=DH), ACT.Copy).then_inc(s_vx, 1)

            def nrow_copy(n, g, bank):
                act.wait_ge(s_ntp, 2 * n + g + 1)
                if not isinstance(n, int) or n > 0:
                    act.wait_ge(s_nst[g], 2 * 16 * n)
                act.activation(nrow[:, g, :], bank[:, :].bitcast(BF16)[0:2 * PART * J, 0:S],
                               ACT.Copy).then_inc(s_nrow, 1)

            def exp(n, c):
                act.wait_ge(s_chunk, CH * n + c + 1)
                k = (CH * n + c - NPR) // 4 if isinstance(n, int) else 8 * n + (c - NPR) // 4
                if not isinstance(n, int) or k >= 0:
                    act.wait_ge(s_pv, k + 1)
                act.activation(probs[c % NPR][:, :], ps_t[bank_of(c)[0]][:, :], ACT.Exp, scale=SCALE).then_inc(s_exp, 1)

            def raw_copy(n, g):
                act.wait_ge(s_pv, 8 * n + 4 * g + 4)
                if not isinstance(n, int) or n > 0 or g > 0:
                    act.wait_ge(s_rt, 2 * n + g)
                act.activation(raw[:, :], ps_pv[:, :], ACT.Copy).then_inc(s_raw, 1)

            def attT_copy(n):
                act.wait_ge(s_atp, n + 1)
                act.activation(attT[:, :], ps_a[:, 0:S], ACT.Copy).then_inc(s_attT, 1)

            def xt2_copy(n):
                act.wait_ge(s_x2p, n + 1)
                if not isinstance(n, int) or n > 0:
                    act.wait_ge(s_x2c, n)
                    act.wait_ge(s_lp, n)
                act.activation(xt2[:, :], ps_a[:, 0:S], ACT.Copy).then_inc(s_x2T, 1)

            def head():
                xnT_copy(0)
                act.wait_ge(s_w, 16 * 4)
                q_copy(0, 0)
                k_copy(0, 0)
                mask_bias(0, 0)
                mask_bias(1, 1)
                act.wait_ge(s_zero, 2)
                v_copy(0, 0)
                xnT_copy(1)
                q_copy(1, 1)
                k_copy(1, 1)
                xnT_copy(2)
                q_copy(2, 0)
                k_copy(2, 0)
                nrow_copy(0, 0, ps_a)

            def exp_gap(k):
                act.wait_ge(s_gap, k + 1)
                ts = ROUTED[k]
                act.activation(egap[:, ts], gap[:, ts], ACT.Exp).then_inc(s_egap, 1)

            def body(i, par):
                for s in range(CH):
                    exp(i, s)
                    if s == 1 and early(i, 6):
                        mask_bias(i + 2, par)
                    if s == 2 and later(i):
                        raw_copy(i - 1, 1)
                    if s == 6 and later(i):
                        attT_copy(i - 1)
                    if s == 10:
                        nrow_copy(i, 1, ps_b)
                    if s == 13 and early(i, 7):
                        v_copy(i + 1, 1 - par)
                    if s == 16 and later(i):
                        xt2_copy(i - 1)
                    if s == 18:
                        raw_copy(i, 0)
                    if s == 21 and early(i, 5):
                        xnT_copy(i + 3)
                    if s == 23 and early(i, 5):
                        q_copy(i + 3, 1 - par)
                    if s == 25 and early(i, 7):
                        nrow_copy(i + 1, 0, ps_a)
                    if s == 26 and early(i, 5):
                        k_copy(i + 3, 1 - par)
                    if s == 24 and not early(i, 7):
                        exp_gap(0)
                    if s in (28, 30) and in_loop(i):
                        h = (s - 28) // 2
                        act.wait_ge(s_wf[h], 16 * i)
                        act.activation(wh[:, bass.ds(2 * (i - 1) + h, 1), :].rearrange("p o n -> p (o n)"), wst[h][:, :],
                                       ACT.Copy).then_inc(s_wh, 1)

            batches(act, head, body)
            raw_copy(B - 1, 1)

            def silu(tc, u, first):
                act.wait_ge(s_g, 2 * E * tc + u + 1)
                if not first:
                    act.wait_ge(s_hid, 2 * E * tc + u - 1)
                act.activation(act_sb[u % 2][:, :], (ps_t, ps_s)[u % 2][0][:, :], ACT.Silu).then_inc(s_act, 1)

            def chunk_of_tokens(tc, first):
                for u in range(FT * E):
                    silu(tc, u, first and u < 2)
                    if first and u == FT * 3 - 1:
                        attT_copy(B - 1)
                    if first and u == FT * 6 - 1:
                        xt2_copy(B - 1)
                    if first and u == FT * 7 - 1:
                        exp_gap(1)

            chunk_of_tokens(0, True)
            with act.Fori(1, TC) as tc:
                chunk_of_tokens(tc, False)

        @block.vector
        def _(dve):
            chain = Chain(s_dve)

            def moments(which, n, done, stages=range(3)):
                src = (x_sb, res)[which]
                for stage in stages:
                    if stage:
                        chain.settle(dve)
                    if stage == 0:
                        for t in range(QT):
                            ins = dve.bn_stats(stats[:, which, t, :], src[:, 2 * n + t, :])
                        chain.mark(ins)
                    elif stage == 1:
                        for t in range(QT):
                            ins = dve.bn_aggr(mv[:, which, t, :], stats[:, which, t, :])
                        chain.mark(ins)
                    else:
                        dve.tensor_scalar(vareps[:, which, :], mv[:, which, :, 1], EPS, None, ALU.add).then_inc(done, 1)

            def scaled(which, src, dst, done):
                for t in range(QT):
                    ins = dve.tensor_scalar(dst[:, t, :], src[t], mv[:, which, t, 0:1], rstd[:, which, t:t + 1],
                                            ALU.subtract, ALU.mult)
                ins.then_inc(done, 1)

            def norm1(n):
                dve.wait_ge(s_rs1, n + 1)
                if not isinstance(n, int) or n > 0:
                    dve.wait_ge(s_xnp, n)
                scaled(0, [x_sb[:, 2 * n + t, :] for t in range(QT)], xn, s_xn)

            def norm2(n):
                dve.wait_ge(s_rs2, n + 1)
                if not isinstance(n, int) or n > 0:
                    dve.wait_ge(s_x2p, n)
                scaled(1, [res[:, 2 * n + t, :] for t in range(QT)], xn2, s_xn2)

            def row_max(n, s):
                g, j, e, t = s // 16, s // 4 % 4, s // 2 % 2, s % 2
                dve.wait_ge(s_tile, TILES * n + s + 1)
                dve.tensor_reduce(nmax[:, g, 2 * t + e, j:j + 1], ps_s[s % NS][:, :], AX.X, ALU.max,
                                  negate=True).then_inc(s_max, 1)

            def max_parts(n, g, stages=range(3)):
                src = nmax[:, g]
                h, m, l = (nsp[:, g, :, a, :] for a in range(PART))
                for stage in stages:
                    if stage == 0:
                        dve.wait_ge(s_max, TILES * n + 16 * (g + 1))
                        if not isinstance(n, int) or n > 0:
                            dve.wait_ge(s_ntp, 2 * n + g - 1)
                        chain.link(dve, dve.tensor_copy(h, src))
                        chain.mark(dve.tensor_tensor(nrest[:, :, :], src, h, ALU.subtract))
                    elif stage == 1:
                        chain.settle(dve)
                        chain.link(dve, dve.tensor_copy(m, nrest[:, :, :]))
                        chain.mark(dve.tensor_tensor(nrest[:, :, :], nrest[:, :, :], m, ALU.subtract))
                    else:
                        chain.settle(dve)
                        dve.tensor_copy(l, nrest[:, :, :]).then_inc(s_nsp, 1)

            def mask_flag(n):
                dve.wait_ge(s_mf, n + 1)
                dve.tensor_scalar(flag[0:1, bass.ds(n, 1)], ps_b[0:1, 0:1], 0.0, None, ALU.is_lt).then_inc(s_flag, 1)

            def normalise(n, g):
                dve.wait_ge(s_rt, 2 * n + g + 1)
                if g == 0 and (not isinstance(n, int) or n > 0):
                    dve.wait_ge(s_atp, n)
                for e in range(2):
                    v = ps_a[:, 2 * P * e:2 * P * (e + 1)].rearrange("q (t j r) -> q t j r", t=QT, j=J)
                    ins = dve.reciprocal(rec[:, e], v[:, :, :, 16 * e + DH])
                chain.link(dve, ins)
                for e in range(2):
                    v = ps_a[:, 2 * P * e:2 * P * (e + 1)].rearrange("q (t j r) -> q t j r", t=QT, j=J)
                    ins = dve.tensor_tensor(
                        att[:, :, e, J * g:J * g + J, :], v[:, :, :, 16 * e:16 * e + DH],
                        rec[:, e].rearrange("q t (j o) -> q t j o", o=1).to_broadcast([P, QT, J, DH]), ALU.mult)
                ins.then_inc(s_att, 1)

            def residual(n):
                dve.wait_ge(s_op, n + 1)
                if isinstance(n, int) and n == 0:
                    dve.wait_ge(s_resx, 1)
                r = res[:, bass.ts(n, QT), :]
                dve.tensor_tensor(r, ps_a[:, 0:QT * D].rearrange("q (t d) -> q t d", t=QT), r, ALU.add).then_inc(s_res, 1)

            def norm2_moments(n, stages):
                if 0 in stages:
                    wait_first(dve, s_res, n + 1)
                moments(1, n, s_mv2, stages)

            def logits_copy(n):
                dve.wait_ge(s_lp, n + 1)
                dve.tensor_copy(logits[:, bass.ts(n, QT), :],
                                ps_a[:, 0:QT * E].rearrange("q (t e) -> q t e", t=QT)).then_inc(s_lg, 1)

            def route_top(k):
                ts = ROUTED[k]
                if k == 0:
                    dve.wait_ge(s_idz, 6)
                dve.wait_ge(s_lg, B - 1 + k)
                for t in range(ts.start, ts.stop):
                    ins = dve.max(top[:, t, :], logits[:, t, :])
                chain.link(dve, ins)
                dve.tensor_tensor(gap[:, ts], top[:, ts, 1], top[:, ts, 0], ALU.subtract).then_inc(s_gap, 1)

            def route(k):
                ts = ROUTED[k]
                for t in range(ts.start, ts.stop):
                    ins = dve.max_index(topi[:, t, :], top[:, t, :], logits[:, t, :])
                if k == 0:
                    ins = dve.tensor_copy(lane[:, :], lanei[:, :])
                chain.link(dve, ins)
                dve.tensor_copy(topf[:, ts, :], topi[:, ts, 0:2])
                dve.wait_ge(s_egap, k + 1)
                chain.link(dve, dve.tensor_scalar(gate[:, 1, ts], egap[:, ts], 1.0, None, ALU.add))
                chain.link(dve, dve.reciprocal(gate[:, 0, ts], gate[:, 1, ts]))
                chain.link(dve, dve.tensor_tensor(gate[:, 1, ts], egap[:, ts], gate[:, 0, ts], ALU.mult))
                shape = [P, ts.stop - ts.start, E]

                def over(ap):
                    return ap.rearrange("q (t o) -> q t o", o=1).to_broadcast(shape)

                for r, c in ((0, comb), (1, comb2)):
                    chain.link(dve, dve.tensor_tensor(c[:, ts, :],
                                                      lane[:, :].rearrange("q (o e) -> q o e", o=1).to_broadcast(shape),
                                                      over(topf[:, ts, r]), ALU.is_equal))
                    chain.link(dve, dve.tensor_tensor(c[:, ts, :], c[:, ts, :], over(gate[:, r, ts]), ALU.mult))
                chain.link(dve, dve.tensor_tensor(comb[:, ts, :], comb[:, ts, :], comb2[:, ts, :], ALU.add))

            def split_first():
                for full, f, o, order in ((s_qf, qf[0], qs, (2, 1, 0)), (s_kf, kf[0], ks, (0, 1, 2))):
                    h, m, l = (o[:, a, :] for a in order)
                    dve.wait_ge(full, 1)
                    ins = dve.tensor_copy(h, f[:, :])
                    ins.then_inc(s_split, 1)
                    dve.wait_ge(s_split, 1 if o is qs else 4)
                    chain.link(dve, dve.tensor_tensor(f[:, :], f[:, :], h, ALU.subtract))
                    dve.tensor_copy(m, f[:, :]).then_inc(s_split, 1)
                    dve.wait_ge(s_split, 2 if o is qs else 5)
                    dve.tensor_tensor(l, f[:, :], m, ALU.subtract).then_inc(s_split, 1)

            def max_at(i, s):
                if s + LEAD < TILES:
                    row_max(i, s + LEAD)
                elif early(i, 7):
                    row_max(i + 1, s + LEAD - TILES)

            def head():
                dve.memset(qst[1][:, :, :, :], 0.0).then_inc(s_zero, 1)
                dve.wait_ge(s_x, 16)
                moments(0, 0, s_mv1)
                dve.memset(onesf[:, :], 1.0).then_inc(s_ones, 1)
                norm1(0)
                dve.memset(qst[0][ROWS:P, :, :, :], 0.0)
                dve.memset(vx[0][:, :, :, :, :], 1.0)
                split_first()
                dve.memset(vx[1][:, :, :, :, :], 1.0).then_inc(s_zero, 1)
                dve.wait_ge(s_x, 32)
                moments(0, 1, s_mv1)
                mask_flag(0)
                mask_flag(1)
                dve.wait_ge(s_ones, 1)
                dve.wait_ge(s_vo, 16 * 5)
                dve.tensor_scalar(bvb[:, :], onesf[:, :], bv_sb[:, 0:1], None, ALU.mult).then_inc(s_bvb, 1)
                norm1(1)
                moments(0, 2, s_mv1)
                dve.wait_ge(s_obp, 1)
                dve.tensor_tensor(obias[:, :], ps_a[:, 0:D], bo_sb[:, :], ALU.add).then_inc(s_ob, 1)
                norm1(2)
                for s in range(LEAD):
                    row_max(0, s)
                    if s in (15, 16):
                        max_parts(0, 0, [0] if s == 15 else [1, 2])

            def body(i, par):
                for s in range(CH):
                    max_at(i, s)
                    if s == 2 and early(i, 6):
                        mask_flag(i + 2)
                    if s == 4 and later(i):
                        normalise(i - 1, 1)
                    if s in (7, 8, 9):
                        max_parts(i, 1, [s - 7])
                    if s == 8 and later(i):
                        residual(i - 1)
                    if s in (10, 11) and later(i):
                        norm2_moments(i - 1, [0] if s == 10 else [1, 2])
                    if s == 13 and later(i):
                        norm2(i - 1)
                    if s in (15, 16) and early(i, 5):
                        moments(0, i + 3, s_mv1, [0] if s == 15 else [1, 2])
                    if s == 19 and early(i, 5):
                        norm1(i + 3)
                    if s == 19 and later(i):
                        logits_copy(i - 1)
                    if s == 20 and not early(i, 7):
                        route_top(0)
                    if s == 22:
                        normalise(i, 0)
                    if s == 24 and not early(i, 7):
                        route(0)
                    if s in (23, 24) and early(i, 7):
                        max_parts(i + 1, 0, [0] if s == 23 else [1, 2])

            batches(dve, head, body, chain, 2 * (1 + 2 + 4 + 2 + 1 + 4))
            def gated(tc, u, first):
                e, f = u // FT, u % FT
                dve.wait_ge(s_act, 2 * E * tc + u + 1)
                dve.wait_ge(s_u, 2 * E * tc + u + 1)
                if not first:
                    dve.wait_ge(s_eo, E * tc + e - 1)
                dve.tensor_tensor(hid[e % 2][f][:, :], (ps_t, ps_s)[u % 2][1][:, :], act_sb[u % 2][:, :],
                                  ALU.mult).then_inc(s_hid, 1)

            def last_tail(e):
                if e == 0:
                    normalise(B - 1, 1)
                elif e == 2:
                    residual(B - 1)
                    norm2_moments(B - 1, range(3))
                elif e == 3:
                    norm2(B - 1)
                elif e == 5:
                    logits_copy(B - 1)
                    route_top(1)

            def weigh(tc, e, first):
                dve.wait_ge(s_eo, E * tc + e + 1)
                if not first:
                    dve.wait_ge(s_sum, E * tc + e - 1)
                c = comb[:, bass.ts(tc, TT), e:e + 1].to_broadcast([P, TT, D])
                dve.tensor_tensor(part[e % 2][:, :].rearrange("q (t d) -> q t d", t=TT), (ps_b, ps_pv)[e % 2][:, :].rearrange("q (t d) -> q t d", t=TT), c,
                                  ALU.mult).then_inc(s_part, 1)

            def chunk_of_tokens(tc, first):
                for e in range(E):
                    for f in range(FT):
                        gated(tc, FT * e + f, first and e < 2)
                    if first and e:
                        last_tail(e - 1)
                    if e:
                        weigh(tc, e - 1, first and e - 1 < 2)
                weigh(tc, E - 1, False)
                if first:
                    route(1)

            chunk_of_tokens(0, True)
            with dve.Fori(1, TC) as tc:
                chunk_of_tokens(tc, False)


def kernel(x, ctx_1024, mask_BxSxS2_bf1, L0_xattn_Wq, L0_xattn_bq, L0_xattn_Wk, L0_xattn_bk, L0_xattn_Wv, L0_xattn_bv,
           L0_xattn_Wo, L0_xattn_bo, L0_ffn_router_w, L0_ffn_w1, L0_ffn_w3, L0_ffn_w2):
    import numpy as np
    import concourse.bacc as bacc
    from concourse.bass_utils import run_bass_kernel_spmd

    def turned(w):
        return np.ascontiguousarray(np.asarray(w).T)

    d = L0_xattn_Wv.shape[0]

    def regrouped(a, order):
        a = np.asarray(a)
        lead = a.shape[:-1]
        axes = tuple(range(len(lead))) + tuple(len(lead) + o for o in order)
        return np.ascontiguousarray(a.reshape(*lead, 2, 8, 8).transpose(axes).reshape(*lead, d))

    def by_two(w):
        return w.reshape(4, 2, *w.shape[1:]).transpose(0, 2, 1, 3).reshape(4, w.shape[1], -1)

    arrays = {
        "x": np.ascontiguousarray(x),
        "ctx_t": np.ascontiguousarray(np.asarray(ctx_1024).transpose(0, 2, 1)),
        "mask": np.ascontiguousarray(mask_BxSxS2_bf1).view(np.uint8),
        "wq_t": regrouped(turned(L0_xattn_Wq), (0, 2, 1)), "bq": regrouped(L0_xattn_bq, (0, 2, 1)),
        "wk_t": regrouped(turned(L0_xattn_Wk), (0, 2, 1)), "bk": regrouped(L0_xattn_bk, (0, 2, 1)),
        "wv_t": regrouped(turned(L0_xattn_Wv), (1, 0, 2)),
        "bv": np.ascontiguousarray(L0_xattn_bv),
        "wo_t": turned(L0_xattn_Wo), "bo": np.ascontiguousarray(L0_xattn_bo),
        "router_w": np.ascontiguousarray(L0_ffn_router_w),
        "w13": np.ascontiguousarray(np.concatenate([by_two(np.asarray(L0_ffn_w1)), by_two(np.asarray(L0_ffn_w3))])),
        "w2": np.ascontiguousarray(L0_ffn_w2),
    }
    nc = bacc.Bacc("TRN2", target_bir_lowering=False, num_devices=1)
    ins = {n: nc.dram_tensor(f"in_{n}", a.shape, mybir.dt.from_np(a.dtype), kind="ExternalInput").ap()
           for n, a in arrays.items()}
    out = nc.dram_tensor("out_x", arrays["x"].shape, F32, kind="ExternalOutput").ap()
    xattn_ffn_kernel(nc, **ins, out=out)
    r = run_bass_kernel_spmd(nc, [{f"in_{n}": a for n, a in arrays.items()}], core_ids=[0])
    return r.results[0]["out_x"]
```

```python
from contextlib import ExitStack

import concourse.bass as bass
from concourse import mybir

ALU = mybir.AluOpType
ACT = mybir.ActivationFunctionType
AX = mybir.AxisListType
F32 = mybir.dt.float32
F32R = mybir.dt.float32r
BF16 = mybir.dt.bfloat16
I32 = mybir.dt.int32
U32 = mybir.dt.uint32

P = 128


def xattn_ffn_kernel(nc: bass.Bass, x, ctx_t, mask, wq_t, bq, wk_t, bk, wv_t, bv, wo_t, bo, router_w, w13, w2, out):
    B, S, D = x.shape
    S2 = ctx_t.shape[2]
    H, DH = 16, 8
    E = router_w.shape[1]
    WP, _, WN = w13.shape
    F = WN // 2
    NP = H // 2
    G = 2
    J = NP // G
    QT = S // P
    KC = S2 // P
    NT = B * QT
    FT = F // P
    PART = 3
    ROWS = 2 * 6 * DH
    KROWS = ROWS + 2 * PART
    CH = G * KC * J
    TILES = G * J * 2 * QT
    NST, NS, NPR = 3, 2, 8
    SHIFT = 14
    SCALE = float(DH) ** -0.5
    MASKED = 1.0e9 * float(DH) ** 0.5
    EPS = 1e-5
    TC = 4
    TT = NT // TC
    ROUTED = slice(0, NT - QT), slice(NT - QT, NT)
    LEAD = CH - 8
    assert CH == 32 and TILES == 32 and ROWS == 96 and QT * P * 2 == 512 and S2 == 512 and E == 8

    x_v = x.rearrange("b (t p) d -> p (b t) d", p=P)
    out_v = out.rearrange("b (t p) d -> p (b t) d", p=P)
    mask_v = mask.rearrange("b (t p) k -> p b t k", p=P)

    with ExitStack() as ctx:
        def sb(name, shape, dt):
            return ctx.enter_context(nc.sbuf_tensor(name, shape, dt))

        def pb(name, shape, dt):
            return ctx.enter_context(nc.psum_tensor(name, shape, dt))

        def sem(name):
            return ctx.enter_context(nc.semaphore(name))

        x_sb = sb("x_sb", [P, NT, D], F32)
        res = sb("res", [P, NT, D], F32)
        ctx_sb = [sb(f"ctx_sb{n}", [P, S2], F32) for n in range(2)]
        mask_sb = sb("mask_sb", [P, 2, QT, S2], mask.dtype)
        mbias = sb("mbias", [P, B, QT, S2], BF16)
        msum = sb("msum", [P, 2], F32)
        flag = sb("flag", [1, B], I32)
        wq_sb = sb("wq_sb", [P, D], F32)
        wk_sb = sb("wk_sb", [P, D], F32)
        wv_sb = sb("wv_sb", [P, D], F32)
        wo_sb = sb("wo_sb", [P, D], F32)
        bq_sb = sb("bq_sb", [P, 1], F32)
        bk_sb = sb("bk_sb", [P, 1], F32)
        bv_sb = sb("bv_sb", [P, 1], F32)
        bo_sb = sb("bo_sb", [P, D], F32)
        bvb = sb("bvb", [P, P], F32)
        obias = sb("obias", [P, D], F32)
        rw_sb = sb("rw_sb", [P, E], F32)
        ident = sb("ident", [P, P], F32)
        identb = sb("identb", [P, P], BF16)
        onesf = sb("onesf", [P, P], F32)
        stats = sb("stats", [P, 2, QT, 6], F32)
        mv = sb("mv", [P, 2, QT, 2], F32)
        vareps = sb("vareps", [P, 2, QT], F32)
        token = sb("token", [P, 32], F32)
        zero = sb("zero", [P, 1], F32)
        minus_half = sb("minus_half", [P, QT], F32)
        rstd = sb("rstd", [P, 2, QT], F32)
        xn = sb("xn", [P, QT, D], F32)
        xnT = sb("xnT", [P, S], F32)
        qf = [sb(f"qf{n}", [P, S], F32) for n in range(2)]
        kf = [sb(f"kf{n}", [P, S2], F32) for n in range(2)]
        qs = sb("qs", [P, PART, S], BF16)
        ks = sb("ks", [P, PART, S2], BF16)
        kst = [sb(f"kst{n}", [P, NP, S2], BF16) for n in range(2)]
        qst = [sb(f"qst{n}", [P, 2, NP, S], BF16) for n in range(2)]
        vx = [sb(f"vx{n}", [P, KC, NP, 2, 16], F32) for n in range(2)]
        nmax = sb("nmax", [P, G, QT * 2, J], F32)
        nrest = sb("nrest", [P, QT * 2, J], F32)
        nsp = sb("nsp", [P, G, QT * 2, PART, J], BF16)
        nrow = sb("nrow", [2 * PART * J, G, S], BF16)
        probs = [sb(f"probs{n}", [P, 2 * S], F32) for n in range(NPR)]
        raw = sb("raw", [P, 2 * S], F32)
        rec = sb("rec", [P, 2, QT, J], F32)
        att = sb("att", [P, QT, 2, NP, DH], F32)
        attT = sb("attT", [P, S], F32)
        xn2 = sb("xn2", [P, QT, D], F32)
        xt2 = sb("xt2", [P, S], F32)
        x2h = sb("x2h", [P, NT * P], F32R)
        x2l = sb("x2l", [P, NT * P], F32R)
        logits = sb("logits", [P, NT, E], F32)
        wst = [sb(f"wst{n}", [P, WN], F32) for n in range(2)]
        wh = sb("wh", [P, WP, WN], F32R)
        wl = sb("wl", [P, WP, WN], F32R)
        w2_sb = sb("w2_sb", [P, E, FT, D], F32)
        top = sb("top", [P, NT, E], F32)
        topi = sb("topi", [P, NT, E], U32)
        topf = sb("topf", [P, NT, 2], F32)
        gap = sb("gap", [P, NT], F32)
        egap = sb("egap", [P, NT], F32)
        gate = sb("gate", [P, 2, NT], F32)
        lane = sb("lane", [P, E], F32)
        lanei = sb("lanei", [P, E], I32)
        comb = sb("comb", [P, NT, E], F32)
        comb2 = top
        act_sb, hid = probs[0:2], (probs[2:4], probs[6:8])
        part = probs[4:6]

        TERMS = ((0, 0, 3), (3, 0, 2), (5, 0, 1)), ((0, 0, 3), (3, 1, 2), (5, 2, 1))
        kd = nc.dram_tensor("k_stack", (6, 2 * DH, NP, S2), BF16, kind="Internal").ap()
        qd = nc.dram_tensor("q_stack", (2, 6, 2, DH, NP, S), BF16, kind="Internal").ap()

        ps_t = [pb(f"ps_t{n}", [P, 512], F32) for n in range(NST)]
        ps_s = [pb(f"ps_s{n}", [P, 512], F32) for n in range(NS)]
        ps_pv = pb("ps_pv", [P, 512], F32)
        ps_a = pb("ps_a", [P, 512], F32)
        ps_b = pb("ps_b", [P, 512], F32)

        s_x = sem("s_x"); s_w = sem("s_w"); s_vo = sem("s_vo")
        s_wf = [sem("s_wf0"), sem("s_wf1")]
        s_w2 = sem("s_w2")
        s_ctx = [sem("s_ctx0"), sem("s_ctx1")]; s_mask = [sem("s_mask0"), sem("s_mask1")]
        s_zero = sem("s_zero"); s_const = sem("s_const"); s_idz = sem("s_idz"); s_ones = sem("s_ones")
        s_bvb = sem("s_bvb"); s_obp = sem("s_obp"); s_ob = sem("s_ob")
        s_resx = sem("s_resx")
        s_wh = sem("s_wh"); s_wl = sem("s_wl")
        s_dve = sem("s_dve"); s_pool = sem("s_pool")
        s_mv1 = sem("s_mv1"); s_xn = sem("s_xn"); s_xnp = sem("s_xnp"); s_xnT = sem("s_xnT")
        s_qp = sem("s_qp"); s_qf = sem("s_qf"); s_kp = sem("s_kp"); s_kf = sem("s_kf")
        s_vp = sem("s_vp"); s_vx = sem("s_vx")
        s_split = sem("s_split"); s_dram = sem("s_dram"); s_stk = [sem("s_stk0"), sem("s_stk1")]
        s_mb = sem("s_mb"); s_mf = sem("s_mf"); s_flag = sem("s_flag")
        s_tile = sem("s_tile"); s_max = sem("s_max"); s_nsp = sem("s_nsp"); s_ntp = sem("s_ntp")
        s_nrow = sem("s_nrow"); s_nst = [sem("s_nst0"), sem("s_nst1")]
        s_chunk = sem("s_chunk"); s_exp = sem("s_exp"); s_pv = sem("s_pv"); s_raw = sem("s_raw"); s_rt = sem("s_rt")
        s_att = sem("s_att"); s_atp = sem("s_atp"); s_attT = sem("s_attT"); s_op = sem("s_op"); s_res = sem("s_res")
        s_mv2 = sem("s_mv2"); s_xn2 = sem("s_xn2"); s_x2p = sem("s_x2p"); s_x2T = sem("s_x2T")
        s_x2h = sem("s_x2h"); s_x2c = sem("s_x2c"); s_lp = sem("s_lp"); s_lg = sem("s_lg")
        s_gap = sem("s_gap"); s_egap = sem("s_egap")
        s_g = sem("s_g"); s_u = sem("s_u"); s_act = sem("s_act"); s_hid = sem("s_hid"); s_eo = sem("s_eo")
        s_part = sem("s_part"); s_sum = sem("s_sum"); s_out = sem("s_out")

        tokens = []

        def carried(eng, s, value):
            eng.wait_ge(s, value)
            if not isinstance(value, int):
                tokens.append(0)
                cell = token[:, len(tokens) - 1:len(tokens)]
                if eng is nc.vector:
                    eng.memset(cell, 0.0)
                else:
                    eng.tensor_tensor(cell, zero[:, 0:1], zero[:, 0:1], ALU.add)

        class Chain:

            def __init__(self, s):
                self.s, self.base, self.n = s, 0, 0

            def mark(self, ins):
                self.n += 1
                ins.then_inc(self.s, 1)

            def settle(self, eng, wait=None):
                if wait is None:
                    eng.wait_ge(self.s, self.base + self.n)
                else:
                    wait(eng, self.s, self.base + self.n)

            def link(self, eng, ins):
                self.mark(ins)
                self.settle(eng)

        def batches(eng, head, body, chain=None, per_pair=0):
            head()
            body(0, 0)
            n0 = chain.n if chain else 0
            with eng.Fori(0, 2) as t:
                if chain:
                    chain.base, chain.n = n0 + t * per_pair, 0
                body(2 * t + 1, 1)
                body(2 * t + 2, 0)
                if chain:
                    assert chain.n == per_pair, chain.n
            if chain:
                chain.base, chain.n = 0, n0 + 2 * per_pair
            for i in (5, 6, 7):
                body(i, i % 2)

        def bank_of(c):
            return (c if c < SHIFT else c + 1) % NST, 2 if c in (SHIFT, SHIFT + 1) else 5 if c == SHIFT + 2 else 3

        PE = dict(mask_sum=3, turn_raw1=4, turn_att=5, out_proj=7, turn_max1=10, v_proj=12, turn_xn2=15,
                  router=19, xn_turn=22, turn_raw0=22, q_proj=23, turn_max0=26, k_proj=27)
        ACTE = dict(mask_bias=0, raw1=1, attT=5, nrow1=10, v=14, xt2=15, raw0=17, xnT=22, q=25,
                    nrow0=26, k=27, upper=(26, 30))
        DVE = dict(flag=4, normalise1=4, residual=7, moments2=(11, 11, 11), moments1=(12, 16, 16),
                   logits=19, normalise0=23)

        def at(steps, s):
            return [k for k, step in enumerate(steps) if step == s]

        def early(i, last):
            return not isinstance(i, int) or i < last

        def in_loop(i):
            return not isinstance(i, int) or 1 <= i < 5

        def later(i, first=1):
            return not isinstance(i, int) or i >= first

        block = ctx.enter_context(nc.Block())

        @block.sync
        def _(sp):
            def load_ctx(n, par):
                sp.dma_start(ctx_sb[par][:, :], ctx_t[n]).then_inc(s_ctx[par], 16)

            def load_mask(n, par):
                sp.dma_start(mask_sb[:, par], mask_v[:, n]).then_inc(s_mask[par], 16)

            def load_both(n, par):
                sp.wait_ge(s_mb, n - 1)
                sp.wait_ge(s_vp, n - 1)
                load_ctx(n, par)
                load_mask(n, par)

            def to_dram(n):
                if not isinstance(n, int) or n > 0:
                    for g in range(G):
                        sp.wait_ge(s_stk[g], 2 * 16 * n)
                sp.wait_ge(s_split, 6 * n + 3)
                for t, a, cnt in TERMS[1]:
                    for e in range(2):
                        sp.dma_start(qd[e, t:t + cnt, e].rearrange("t d p n -> (d p) t n"),
                                     qs[64 * e:64 * e + 64, a:a + cnt, :]).then_inc(s_dram, 16)
                sp.wait_ge(s_split, 6 * n + 6)
                for t, a, cnt in TERMS[0]:
                    sp.dma_start(kd[t:t + cnt].rearrange("t r p n -> (r p) t n"), ks[:, a:a + cnt, :]).then_inc(s_dram, 16)
                sp.wait_ge(s_dram, 16 * (9 * n + 11))

            def stack(n, g, par):
                if not isinstance(n, int) or n >= 2:
                    sp.wait_ge(s_chunk, CH * (n - 2) + CH // G * (g + 1))
                ps = slice(J * g, J * g + J)
                sp.dma_start(kst[par][0:ROWS, ps, :],
                             kd[:, :, ps].rearrange("t r p n -> (t r) p n")).then_inc(s_stk[g], 16)
                sp.dma_start(qst[par][0:ROWS, :, ps, :].rearrange("r e p n -> r e (p n)"),
                             qd[:, :, :, :, ps].rearrange("s t e d p n -> (t e d) s (p n)")).then_inc(s_stk[g], 16)

            def max_rows(n, g, par):
                sp.wait_ge(s_nrow, 2 * n + g + 1)
                for e in range(2):
                    r = PART * e
                    sp.dma_start(qst[par][ROWS + r:ROWS + r + PART, e, J * g:J * g + J, :],
                                 nrow[J * r:J * (r + PART), g, :]).then_inc(s_nst[g], 16)

            def head():
                sp.dma_start(x_sb[:, 0:QT, :], x_v[:, 0:QT, :]).then_inc(s_x, 16)
                sp.dma_start(wq_sb[:, :], wq_t).then_inc(s_w, 16)
                sp.dma_start(bq_sb[:, :], bq.rearrange("(p o) -> p o", o=1)).then_inc(s_w, 16)
                load_ctx(0, 0)
                sp.dma_start(wk_sb[:, :], wk_t).then_inc(s_w, 16)
                sp.dma_start(bk_sb[:, :], bk.rearrange("(p o) -> p o", o=1)).then_inc(s_w, 16)
                sp.wait_ge(s_zero, 1)
                for e in range(2):
                    sp.dma_start(qd[e, :, 1 - e].rearrange("t d p n -> t d (p n)"),
                                 qst[1][0:6 * DH, 0, :, :].rearrange("r p n -> r (p n)")).then_inc(s_dram, 16)
                load_mask(0, 0)
                sp.wait_ge(s_x, 16)
                sp.dma_start(x_sb[:, QT:NT, :], x_v[:, QT:NT, :]).then_inc(s_x, 16)
                for dst, src in ((wv_sb, wv_t), (wo_sb, wo_t), (rw_sb, router_w)):
                    sp.dma_start(dst[:, :], src).then_inc(s_vo, 16)
                sp.dma_start(bv_sb[:, :], bv.rearrange("(p o) -> p o", o=1)).then_inc(s_vo, 16)
                sp.dma_start(bo_sb[:, :], bo.rearrange("(o d) -> o d", o=1).partition_broadcast(P)).then_inc(s_vo, 16)
                load_mask(1, 1)
                load_ctx(1, 1)
                sp.wait_ge(s_dram, 32)
                to_dram(0)
                stack(0, 0, 0)
                stack(0, 1, 0)
                load_both(2, 0)
                to_dram(1)
                max_rows(0, 0, 0)
                stack(1, 0, 1)

            def weights(i):
                for h in range(2):
                    sp.dma_start(wst[h][:, :], w13[2 * (i - 1) + h]).then_inc(s_wf[h], 16)

            def body(i, par):
                if early(i, 7):
                    stack(i + 1, 1, 1 - par)
                max_rows(i, 1, par)
                if early(i, 5):
                    load_both(i + 3, 1 - par)
                if early(i, 6):
                    to_dram(i + 2)
                if in_loop(i):
                    weights(i)
                if early(i, 7):
                    max_rows(i + 1, 0, 1 - par)
                if early(i, 6):
                    stack(i + 2, 0, par)

            batches(sp, head, body)
            sp.dma_start(w2_sb[:, :, :, :], w2.rearrange("e (f p) d -> p e f d", p=P)).then_inc(s_w2, 16)
            with sp.Fori(0, TC) as tc:
                sp.wait_ge(s_sum, E * tc + E)
                sp.dma_start(out_v[:, bass.ts(tc, TT), :], res[:, bass.ts(tc, TT), :]).then_inc(s_out, 16)
            sp.wait_ge(s_out, 16 * TC)

        @block.gpsimd
        def _(pool):
            chain = Chain(s_pool)

            def norm(which, n):
                src, dst, moments, done, turned = ((x_sb, xn, s_mv1, s_xn, s_xnp), (res, xn2, s_mv2, s_xn2, s_x2p))[which]

                def over(ap):
                    return ap.rearrange("p (t o) -> p t o", o=1).to_broadcast([P, QT, D])

                pool.wait_ge(moments, n + 1)
                chain.mark(pool.tensor_tensor(rstd[:, which, :], vareps[:, which, :], minus_half[:, :], ALU.pow))
                if which == 0 and later(n):
                    pool.wait_ge(turned, n)
                chain.link(pool, pool.tensor_tensor(dst[:, :, :], src[:, bass.ts(n, QT), :], over(mv[:, which, :, 0]),
                                                    ALU.subtract))
                pool.tensor_tensor(dst[:, :, :], dst[:, :, :], over(rstd[:, which, :]), ALU.mult).then_inc(done, 1)

            def rounded(dst, src):
                z = zero[:, 0:1]
                if len(src.shape) == 3:
                    z = zero[:, 0:1].rearrange("p (o n) -> p o n", o=1)
                return pool.tensor_tensor(dst, src, z.to_broadcast(list(src.shape)), ALU.add)

            def max_parts(n, g):
                pool.wait_ge(s_max, TILES * n + 16 * (g + 1))
                if later(n):
                    pool.wait_ge(s_ntp, 2 * n + g - 1)
                src = nmax[:, g]
                h, m, l = (nsp[:, g, :, a, :] for a in range(PART))
                chain.link(pool, rounded(h, src))
                chain.link(pool, pool.tensor_tensor(nrest[:, :, :], src, h, ALU.subtract))
                chain.link(pool, rounded(m, nrest[:, :, :]))
                chain.link(pool, pool.tensor_tensor(nrest[:, :, :], nrest[:, :, :], m, ALU.subtract))
                rounded(l, nrest[:, :, :]).then_inc(s_nsp, 1)

            def split(n, par, between):
                pool.wait_ge(s_dram, 16 * (9 * n + 2))
                for full, f, o, order in ((s_qf, qf[par], qs, (2, 1, 0)), (s_kf, kf[par], ks, (0, 1, 2))):
                    h, m, l = (o[:, a, :] for a in order)
                    done = 6 * n + (0 if o is qs else 3)
                    pool.wait_ge(full, n + 1)
                    rounded(h, f[:, :]).then_inc(s_split, 1)
                    pool.wait_ge(s_split, done + 1)
                    chain.link(pool, pool.tensor_tensor(f[:, :], f[:, :], h, ALU.subtract))
                    if o is ks:
                        between()
                    rounded(m, f[:, :]).then_inc(s_split, 1)
                    pool.wait_ge(s_split, done + 2)
                    pool.tensor_tensor(l, f[:, :], m, ALU.subtract).then_inc(s_split, 1)

            def head():
                pool.memset(zero[:, :], 0.0)
                pool.memset(minus_half[:, :], -0.5).then_inc(s_idz, 1)
                pool.memset(ident[:, :], 0.0).then_inc(s_idz, 1)
                pool.memset(identb[:, :], 0.0).then_inc(s_idz, 1)
                pool.wait_ge(s_idz, 3)
                for n, t in enumerate((ident, identb)):
                    pool.affine_select(out=t[:, :], in_=t[:, :], compare_op=ALU.not_equal, fill=1.0, base=0,
                                       pattern=[[-1, P]], channel_multiplier=1).then_inc(s_idz, 1)
                pool.iota(lanei[:, :], pattern=[[1, E]], base=0, channel_multiplier=0).then_inc(s_idz, 1)
                norm(0, 0)
                pool.wait_ge(s_xn, 1)
                for n in range(2):
                    pool.memset(kst[n][ROWS:P, :, :], 1.0).then_inc(s_const, 1)
                pool.wait_ge(s_const, 2)
                norm(0, 1)
                norm(0, 2)
                split(1, 1, lambda: None)
                pool.wait_ge(s_ob, 1)
                pool.wait_ge(s_x, 32)
                pool.tensor_tensor(res[:, :, :], x_sb[:, :, :],
                                   obias[:, :].rearrange("p (o d) -> p o d", o=1).to_broadcast([P, NT, D]),
                                   ALU.add).then_inc(s_resx, 1)
                max_parts(0, 0)

            def x2_parts(n):
                carried(pool, s_x2T, n + 1)
                pool.tensor_copy(x2h[:, bass.ts(n, S)], xt2[:, :]).then_inc(s_x2h, 1)
                carried(pool, s_x2h, n + 1)
                pool.tensor_tensor(x2l[:, bass.ts(n, S)], xt2[:, :], x2h[:, bass.ts(n, S)], ALU.subtract).then_inc(s_x2c, 1)

            def body(i, par):
                def second():
                    max_parts(i, 1)
                    if later(i):
                        norm(1, i - 1)

                if early(i, 6):
                    split(i + 2, par, second)
                else:
                    second()
                if early(i, 5):
                    norm(0, i + 3)
                if later(i):
                    x2_parts(i - 1)
                if early(i, 7):
                    max_parts(i + 1, 0)
                if in_loop(i):
                    for h in range(2):
                        m = 2 * (i - 1) + h
                        carried(pool, s_wh, m + 1)
                        pool.tensor_tensor(wl[:, bass.ds(m, 1), :].rearrange("p o n -> p (o n)"), wst[h][:, :],
                                           wh[:, bass.ds(m, 1), :].rearrange("p o n -> p (o n)"),
                                           ALU.subtract).then_inc(s_wl, 1)

            batches(pool, head, body, chain, 2 * (2 + 4 + 4 + 2 + 2))
            for tc in range(TC):
                for e in range(E):
                    if tc == 0 and e == 2:
                        norm(1, B - 1)
                    if tc == 0 and e == 4:
                        x2_parts(B - 1)
                    pool.wait_ge(s_part, E * tc + e + 1)
                    if e or tc:
                        pool.wait_ge(s_sum, E * tc + e)
                    r = res[:, tc * TT:(tc + 1) * TT, :]
                    pool.tensor_tensor(r, r, part[e % 2][:, :].rearrange("q (t d) -> q t d", t=TT), ALU.add).then_inc(s_sum, 1)

        @block.tensor
        def _(pe):
            def xn_turn(n):
                pe.wait_ge(s_xn, n + 1)
                for t in range(QT):
                    ins = pe.transpose(ps_b[:, t * P:(t + 1) * P], xn[:, t, :], ident[:, :])
                ins.then_inc(s_xnp, 1)

            def q_proj(n):
                pe.wait_ge(s_xnT, n + 1)
                pe.matmul(ps_b[:, 0:S], wq_sb[:, :], xnT[:, :], start=True, stop=True).then_inc(s_qp, 1)

            def k_proj(n, par):
                pe.wait_ge(s_qf, n + 1)
                pe.wait_ge(s_ctx[par], 8 * (n - par) + 16)
                pe.matmul(ps_b[:, :], wk_sb[:, :], ctx_sb[par][:, :], start=True, stop=True).then_inc(s_kp, 1)

            def v_proj(n, par):
                for c in range(KC):
                    ins = pe.matmul(ps_b[:, c * D:(c + 1) * D], ctx_sb[par][:, c * P:(c + 1) * P], wv_sb[:, :],
                                    start=True, stop=True)
                ins.then_inc(s_vp, 1)

            def mask_sum(n, par):
                pe.wait_ge(s_mb, n + 1)
                both = not isinstance(n, int) or n > 0
                if both:
                    pe.matmul(ps_b[0:1, 0:1], msum[:, 1 - par:2 - par], onesf[:, 0:1], start=True, stop=False)
                pe.matmul(ps_b[0:1, 0:1], msum[:, par:par + 1], onesf[:, 0:1], start=not both, stop=True).then_inc(s_mf, 1)

            def turn_max(n, g, bank):
                pe.wait_ge(s_nsp, 2 * n + g + 1)
                for t in range(QT):
                    ins = pe.transpose(bank[:, :].bitcast(BF16)[0:2 * PART * J, t * P:(t + 1) * P],
                                       nsp[:, g, 2 * t:2 * t + 2].rearrange("p e a j -> p (e a j)"), identb[:, :])
                ins.then_inc(s_ntp, 1)

            def tile(n, s, par, masked):
                g, j, e, t = s // 16, s // 4 % 4, s // 2 % 2, s % 2
                p = J * g + j
                if s % 16 == 0:
                    pe.wait_ge(s_stk[g], 2 * 16 * (n + 1))
                if not isinstance(n, int) or n > 0 or s >= NS:
                    pe.wait_ge(s_max, TILES * n + s - NS + 1)
                ins = pe.matmul(ps_s[s % NS][:, :], qst[par][0:ROWS, e, p, t * P:(t + 1) * P], kst[par][0:ROWS, p, :],
                                start=True, stop=not masked)
                if masked:
                    ins = pe.matmul(ps_s[s % NS][:, :], identb[:, :], mbias[:, n, t, :], start=False, stop=True)
                ins.then_inc(s_tile, 1)

            def chunk(n, c, par, masked):
                g, kc, j = c // 16, c // 4 % 4, c % 4
                p = J * g + j
                if c % 16 == 0:
                    pe.wait_ge(s_nst[g], 2 * 16 * (n + 1))
                if not isinstance(n, int) or n > 0 or c >= NST:
                    pe.wait_ge(s_exp, CH * n + c - bank_of(c)[1] + 1)
                bank = ps_t[bank_of(c)[0]]
                ks_ = slice(kc * P, (kc + 1) * P)
                ins = pe.matmul(bank[:, :].rearrange("k (e q) -> k e q", e=2), kst[par][0:KROWS, p, ks_],
                                qst[par][0:KROWS, :, p, :], start=True, stop=not masked)
                if masked:
                    for t in range(QT):
                        ins = pe.matmul(
                            bank[:, :].rearrange("k (e t q) -> k t e q", e=2, t=QT)[:, t],
                            mbias[:, n, t, ks_],
                            identb[:, :].rearrange("p (o q) -> p o q", o=1).to_broadcast([P, 2, P]),
                            start=False, stop=(t == QT - 1))
                ins.then_inc(s_chunk, 1)

            def values(n, k, par):
                g, kc = k // 4, k % 4
                pe.wait_ge(s_exp, CH * n + 4 * k + 4)
                if k == 0:
                    pe.wait_ge(s_vx, n + 1)
                if kc == 0 and (not isinstance(n, int) or n > 0 or g > 0):
                    pe.wait_ge(s_raw, 2 * n + g)
                for j in range(J):
                    ins = pe.matmul(ps_pv[32 * j:32 * j + 32, :],
                                    vx[par][:, kc, J * g + j].rearrange("k e d -> k (e d)"),
                                    probs[(4 * k + j) % NPR][:, :], start=(kc == 0), stop=(kc == KC - 1))
                ins.then_inc(s_pv, 1)

            def turn_raw(n, g):
                pe.wait_ge(s_raw, 2 * n + g + 1)
                for a in range(2 * QT):
                    ins = pe.transpose(ps_a[:, a * P:(a + 1) * P], raw[:, a * P:(a + 1) * P], ident[:, :])
                ins.then_inc(s_rt, 1)

            def turn_att(n):
                pe.wait_ge(s_att, 2 * n + 2)
                for t in range(QT):
                    ins = pe.transpose(ps_a[:, t * P:(t + 1) * P], att[:, t].rearrange("q e p d -> q (e p d)"),
                                       ident[:, :])
                ins.then_inc(s_atp, 1)

            def out_proj(n):
                pe.wait_ge(s_attT, n + 1)
                for t in range(QT):
                    ins = pe.matmul(ps_a[:, t * D:(t + 1) * D], attT[:, t * P:(t + 1) * P], wo_sb[:, :],
                                    start=True, stop=True)
                ins.then_inc(s_op, 1)

            def turn_xn2(n):
                pe.wait_ge(s_xn2, n + 1)
                for t in range(QT):
                    ins = pe.transpose(ps_a[:, t * P:(t + 1) * P], xn2[:, t, :], ident[:, :])
                ins.then_inc(s_x2p, 1)

            def router(n):
                pe.wait_ge(s_x2T, n + 1)
                for t in range(QT):
                    ins = pe.matmul(ps_a[:, t * E:(t + 1) * E], xt2[:, t * P:(t + 1) * P], rw_sb[:, :],
                                    start=True, stop=True)
                ins.then_inc(s_lp, 1)

            def tile_at(i, par, s, masked):
                if s + LEAD < TILES:
                    tile(i, s + LEAD, par, masked)
                elif early(i, 7):
                    tile(i + 1, s + LEAD - TILES, 1 - par, masked)

            def steps(i, par, masked):
                for s in range(CH):
                    chunk(i, s, par, masked)
                    tile_at(i, par, s, masked)
                    if s % 4 == 1 and s > 1:
                        values(i, s // 4 - 1, par)
                    if s == 1 and later(i):
                        values(i - 1, 7, 1 - par)
                    if s == PE["mask_sum"] and early(i, 6):
                        pe.wait_ge(s_kf, i + 3)
                        mask_sum(i + 2, par)
                    if s == PE["turn_raw1"] and later(i):
                        pe.wait_ge(s_nrow, 2 * i + 1)
                        turn_raw(i - 1, 1)
                    if s == PE["turn_att"] and later(i):
                        turn_att(i - 1)
                    if s == PE["out_proj"] and later(i):
                        out_proj(i - 1)
                    if s == PE["turn_max1"]:
                        if early(i, 6):
                            pe.wait_ge(s_flag, i + 3)
                        turn_max(i, 1, ps_b)
                    if s == PE["turn_xn2"] and later(i):
                        pe.wait_ge(s_res, i)
                        turn_xn2(i - 1)
                    if s == PE["v_proj"] and early(i, 7):
                        pe.wait_ge(s_nrow, 2 * i + 2)
                        v_proj(i + 1, 1 - par)
                    if s == PE["router"] and later(i):
                        router(i - 1)
                    if s == PE["xn_turn"] and early(i, 5):
                        pe.wait_ge(s_vx, i + 2)
                        xn_turn(i + 3)
                    if s == PE["q_proj"] and early(i, 5):
                        q_proj(i + 3)
                    if s == PE["turn_raw0"]:
                        if later(i):
                            pe.wait_ge(s_lg, i)
                        else:
                            pe.wait_ge(s_nrow, 1)
                        turn_raw(i, 0)
                    if s == PE["k_proj"] and early(i, 5):
                        k_proj(i + 3, 1 - par)
                    if s == PE["turn_max0"] and early(i, 7):
                        pe.wait_ge(s_att, 2 * i + 1)
                        turn_max(i + 1, 0, ps_a)

            def either(cond, emit):
                with pe.If(cond > 0):
                    emit(True)
                with pe.Else():
                    emit(False)

            def head():
                pe.wait_ge(s_idz, 6)
                xn_turn(0)
                pe.wait_ge(s_w, 16 * 4)
                q_proj(0)
                k_proj(0, 0)
                pe.wait_ge(s_kf, 1)
                pe.wait_ge(s_ones, 1)
                mask_sum(0, 0)
                pe.wait_ge(s_flag, 1)
                mask_sum(1, 1)
                pe.wait_ge(s_vo, 16 * 5)
                pe.wait_ge(s_flag, 2)
                v_proj(0, 0)
                pe.wait_ge(s_bvb, 1)
                pe.matmul(ps_a[:, 0:D], bvb[:, :], wo_sb[:, :], start=True, stop=True).then_inc(s_obp, 1)
                pe.wait_ge(s_vx, 1)
                xn_turn(1)
                q_proj(1)
                pe.wait_ge(s_const, 2)

                def first_tiles(masked):
                    for s in range(LEAD):
                        tile(0, s, 0, masked)
                        if s == 1:
                            k_proj(1, 1)
                        if s == 17:
                            pe.wait_ge(s_ob, 1)
                            turn_max(0, 0, ps_a)
                        if s == 18:
                            pe.wait_ge(s_kf, 2)
                            xn_turn(2)
                        if s == 20:
                            q_proj(2)
                        if s == 22:
                            k_proj(2, 0)

                either(pe.value_load(flag[0:1, 0:1]), first_tiles)

            def body(i, par):
                last = i + 1 if early(i, 7) else i
                either(pe.value_load(flag[0:1, bass.ds(last, 1)]), lambda masked: steps(i, par, masked))

            batches(pe, head, body)
            values(B - 1, 7, (B - 1) % 2)
            gu = [(ps_t[0], ps_t[1]), (ps_s[0], ps_s[1])]
            eo = [ps_b, ps_pv]
            pe.wait_ge(s_wl, WP)
            pe.wait_ge(s_w2, 16)
            pe.wait_ge(s_x2c, B - 1)
            pe.wait_ge(s_exp, CH * B)
            pe.wait_ge(s_max, TILES * B)
            WE = WP // 2

            def up(tc, e, first):
                xh, xl = x2h[:, bass.ts(tc, TT * P)], x2l[:, bass.ts(tc, TT * P)]
                for f in range(FT):
                    u = FT * e + f
                    col = (e % 2) * F + f * P
                    if not first or u >= 2:
                        pe.wait_ge(s_act, FT * E * tc + u - 1)
                    for k, (w, y) in enumerate(((wh, xh), (wl, xh), (wh, xl))):
                        ins = pe.matmul(gu[f][0][:, :], w[:, e // 2, col:col + P], y, start=(k == 0), stop=(k == 2))
                    ins.then_inc(s_g, 1)
                    if not first or u >= 2:
                        pe.wait_ge(s_hid, FT * E * tc + u - 1)
                    for k, (w, y) in enumerate(((wh, xh), (wl, xh), (wh, xl))):
                        ins = pe.matmul(gu[f][1][:, :], w[:, WE + e // 2, col:col + P], y, start=(k == 0), stop=(k == 2))
                    ins.then_inc(s_u, 1)

            def down(tc, e, first):
                pe.wait_ge(s_hid, FT * (E * tc + e + 1))
                if not first or e >= 2:
                    pe.wait_ge(s_part, E * tc + e - 1)
                elif e == 1:
                    pe.wait_ge(s_raw, 2 * B)
                for t in range(TT):
                    for f in range(FT):
                        ins = pe.matmul(eo[e % 2][:, t * D:(t + 1) * D], hid[e % 2][f][:, t * P:(t + 1) * P],
                                        w2_sb[:, e, f, :], start=(f == 0), stop=(f == FT - 1))
                ins.then_inc(s_eo, 1)

            def last_tail(e):
                if e == 0:
                    pe.wait_ge(s_att, 2 * B - 1)
                    turn_raw(B - 1, 1)
                elif e == 1:
                    turn_att(B - 1)
                elif e == 2:
                    out_proj(B - 1)
                elif e == 4:
                    pe.wait_ge(s_res, B)
                    turn_xn2(B - 1)
                elif e == 5:
                    router(B - 1)

            def chunk_of_tokens(tc, first):
                up(tc, 0, first)
                for e in range(E):
                    if e + 1 < E:
                        up(tc, e + 1, first)
                    if first:
                        last_tail(e)
                    down(tc, e, first)

            chunk_of_tokens(0, True)
            pe.wait_ge(s_x2c, B)
            with pe.Fori(1, TC) as tc:
                chunk_of_tokens(tc, False)

        @block.scalar
        def _(act):
            def mask_bias(n, par):
                act.wait_ge(s_mask[par], 8 * (n - par) + 16)
                if not isinstance(n, int) or n >= 2:
                    act.wait_ge(s_mf, n)
                act.activation(mbias[:, n], mask_sb[:, par], ACT.Copy, bias=-MASKED, scale=MASKED,
                               accum_out=msum[:, par:par + 1]).then_inc(s_mb, 1)

            def xnT_copy(n):
                act.wait_ge(s_xnp, n + 1)
                act.activation(xnT[:, :], ps_b[:, 0:S], ACT.Copy).then_inc(s_xnT, 1)

            def q_copy(n, par):
                act.wait_ge(s_qp, n + 1)
                if not isinstance(n, int) or n >= 2:
                    act.wait_ge(s_split, 6 * (n - 2) + 3)
                act.activation(qf[par][:, :], ps_b[:, 0:S], ACT.Identity, bias=bq_sb[:, :]).then_inc(s_qf, 1)

            def k_copy(n, par):
                act.wait_ge(s_kp, n + 1)
                if not isinstance(n, int) or n >= 2:
                    act.wait_ge(s_split, 6 * (n - 2) + 6)
                act.activation(kf[par][:, :], ps_b[:, :], ACT.Identity, bias=bk_sb[:, :]).then_inc(s_kf, 1)

            def v_copy(n, par):
                act.wait_ge(s_vp, n + 1)
                if not isinstance(n, int) or n >= 2:
                    act.wait_ge(s_pv, 8 * (n - 1))
                act.activation(vx[par][:, :, :, :, 0:DH].rearrange("k c p e d -> k (c p e) d"),
                               ps_b[:, :].rearrange("k (h d) -> k h d", d=DH), ACT.Copy).then_inc(s_vx, 1)

            def nrow_copy(n, g, bank):
                act.wait_ge(s_ntp, 2 * n + g + 1)
                if not isinstance(n, int) or n > 0:
                    act.wait_ge(s_nst[g], 2 * 16 * n)
                act.activation(nrow[:, g, :], bank[:, :].bitcast(BF16)[0:2 * PART * J, 0:S],
                               ACT.Copy).then_inc(s_nrow, 1)

            def exp(n, c):
                act.wait_ge(s_chunk, CH * n + c + 1)
                k = (CH * n + c - NPR) // 4 if isinstance(n, int) else 8 * n + (c - NPR) // 4
                if not isinstance(n, int) or k >= 0:
                    act.wait_ge(s_pv, k + 1)
                act.activation(probs[c % NPR][:, :], ps_t[bank_of(c)[0]][:, :], ACT.Exp, scale=SCALE).then_inc(s_exp, 1)

            def raw_copy(n, g):
                act.wait_ge(s_pv, 8 * n + 4 * g + 4)
                if not isinstance(n, int) or n > 0 or g > 0:
                    act.wait_ge(s_rt, 2 * n + g)
                act.activation(raw[:, :], ps_pv[:, :], ACT.Copy).then_inc(s_raw, 1)

            def attT_copy(n):
                act.wait_ge(s_atp, n + 1)
                act.activation(attT[:, :], ps_a[:, 0:S], ACT.Copy).then_inc(s_attT, 1)

            def xt2_copy(n):
                act.wait_ge(s_x2p, n + 1)
                act.activation(xt2[:, :], ps_a[:, 0:S], ACT.Copy).then_inc(s_x2T, 1)

            def head():
                xnT_copy(0)
                act.wait_ge(s_w, 16 * 4)
                q_copy(0, 0)
                k_copy(0, 0)
                mask_bias(0, 0)
                mask_bias(1, 1)
                act.wait_ge(s_zero, 2)
                v_copy(0, 0)
                xnT_copy(1)
                q_copy(1, 1)
                k_copy(1, 1)
                nrow_copy(0, 0, ps_a)
                xnT_copy(2)
                q_copy(2, 0)
                k_copy(2, 0)

            def exp_gap(k):
                act.wait_ge(s_gap, k + 1)
                ts = ROUTED[k]
                act.activation(egap[:, ts], gap[:, ts], ACT.Exp).then_inc(s_egap, 1)

            def body(i, par):
                for s in range(CH):
                    exp(i, s)
                    if s == ACTE["mask_bias"] and early(i, 6):
                        mask_bias(i + 2, par)
                    if s == ACTE["raw1"] and later(i):
                        raw_copy(i - 1, 1)
                    if s == ACTE["attT"] and later(i):
                        attT_copy(i - 1)
                    if s == ACTE["nrow1"]:
                        nrow_copy(i, 1, ps_b)
                    if s == ACTE["v"] and early(i, 7):
                        v_copy(i + 1, 1 - par)
                    if s == ACTE["xt2"] and later(i):
                        xt2_copy(i - 1)
                    if s == ACTE["raw0"]:
                        raw_copy(i, 0)
                    if s == ACTE["xnT"] and early(i, 5):
                        xnT_copy(i + 3)
                    if s == ACTE["q"] and early(i, 5):
                        q_copy(i + 3, 1 - par)
                    if s == ACTE["nrow0"] and early(i, 7):
                        nrow_copy(i + 1, 0, ps_a)
                    if s == ACTE["k"] and early(i, 5):
                        k_copy(i + 3, 1 - par)
                    if s == 24 and not early(i, 7):
                        exp_gap(0)
                    if s in ACTE["upper"] and in_loop(i):
                        h = ACTE["upper"].index(s)
                        act.wait_ge(s_wf[h], 16 * i)
                        act.activation(wh[:, bass.ds(2 * (i - 1) + h, 1), :].rearrange("p o n -> p (o n)"), wst[h][:, :],
                                       ACT.Copy).then_inc(s_wh, 1)

            batches(act, head, body)
            raw_copy(B - 1, 1)

            def silu(tc, u, first):
                act.wait_ge(s_g, 2 * E * tc + u + 1)
                if not first:
                    act.wait_ge(s_hid, 2 * E * tc + u - 1)
                act.activation(act_sb[u % 2][:, :], (ps_t, ps_s)[u % 2][0][:, :], ACT.Silu).then_inc(s_act, 1)

            def chunk_of_tokens(tc, first):
                for u in range(FT * E):
                    silu(tc, u, first and u < 2)
                    if first and u == FT * 3 - 1:
                        attT_copy(B - 1)
                    if first and u == FT * 6 - 1:
                        xt2_copy(B - 1)
                    if first and u == FT * 7 - 1:
                        exp_gap(1)

            chunk_of_tokens(0, True)
            with act.Fori(1, TC) as tc:
                chunk_of_tokens(tc, False)

        @block.vector
        def _(dve):
            chain = Chain(s_dve)

            def moments(which, n, done, stages=range(3)):
                src = (x_sb, res)[which]
                for stage in stages:
                    if stage:
                        if which == 0 and stage == 1 and later(n):
                            dve.wait_ge(s_xn, n)
                        chain.settle(dve, carried if stage == 1 else None)
                    if stage == 0:
                        for t in range(QT):
                            ins = dve.bn_stats(stats[:, which, t, :], src[:, 2 * n + t, :])
                        chain.mark(ins)
                    elif stage == 1:
                        for t in range(QT):
                            ins = dve.bn_aggr(mv[:, which, t, :], stats[:, which, t, :])
                        chain.mark(ins)
                    else:
                        dve.tensor_scalar(vareps[:, which, :], mv[:, which, :, 1], EPS, None, ALU.add).then_inc(done, 1)

            def row_max(n, s):
                g, j, e, t = s // 16, s // 4 % 4, s // 2 % 2, s % 2
                dve.wait_ge(s_tile, TILES * n + s + 1)
                dve.tensor_reduce(nmax[:, g, 2 * t + e, j:j + 1], ps_s[s % NS][:, :], AX.X, ALU.max,
                                  negate=True).then_inc(s_max, 1)

            def mask_flag(n):
                dve.wait_ge(s_mf, n + 1)
                dve.tensor_scalar(flag[0:1, bass.ds(n, 1)], ps_b[0:1, 0:1], 0.0, None, ALU.is_lt).then_inc(s_flag, 1)

            def normalise(n, g):
                dve.wait_ge(s_rt, 2 * n + g + 1)
                if g == 0 and (not isinstance(n, int) or n > 0):
                    dve.wait_ge(s_atp, n)
                for e in range(2):
                    v = ps_a[:, 2 * P * e:2 * P * (e + 1)].rearrange("q (t j r) -> q t j r", t=QT, j=J)
                    ins = dve.reciprocal(rec[:, e], v[:, :, :, 16 * e + DH])
                chain.link(dve, ins)
                for e in range(2):
                    v = ps_a[:, 2 * P * e:2 * P * (e + 1)].rearrange("q (t j r) -> q t j r", t=QT, j=J)
                    ins = dve.tensor_tensor(
                        att[:, :, e, J * g:J * g + J, :], v[:, :, :, 16 * e:16 * e + DH],
                        rec[:, e].rearrange("q t (j o) -> q t j o", o=1).to_broadcast([P, QT, J, DH]), ALU.mult)
                ins.then_inc(s_att, 1)

            def residual(n):
                dve.wait_ge(s_op, n + 1)
                r = res[:, bass.ts(n, QT), :]
                dve.tensor_tensor(r, ps_a[:, 0:QT * D].rearrange("q (t d) -> q t d", t=QT), r, ALU.add).then_inc(s_res, 1)

            def norm2_moments(n, stages):
                if 0 in stages:
                    carried(dve, s_res, n + 1)
                moments(1, n, s_mv2, stages)

            def logits_copy(n):
                dve.wait_ge(s_lp, n + 1)
                dve.tensor_copy(logits[:, bass.ts(n, QT), :],
                                ps_a[:, 0:QT * E].rearrange("q (t e) -> q t e", t=QT)).then_inc(s_lg, 1)

            def route_top(k):
                ts = ROUTED[k]
                if k == 0:
                    dve.wait_ge(s_idz, 6)
                dve.wait_ge(s_lg, B - 1 + k)
                for t in range(ts.start, ts.stop):
                    ins = dve.max(top[:, t, :], logits[:, t, :])
                chain.link(dve, ins)
                dve.tensor_tensor(gap[:, ts], top[:, ts, 1], top[:, ts, 0], ALU.subtract).then_inc(s_gap, 1)

            def route(k):
                ts = ROUTED[k]
                for t in range(ts.start, ts.stop):
                    ins = dve.max_index(topi[:, t, :], top[:, t, :], logits[:, t, :])
                if k == 0:
                    ins = dve.tensor_copy(lane[:, :], lanei[:, :])
                chain.link(dve, ins)
                dve.tensor_copy(topf[:, ts, :], topi[:, ts, 0:2])
                dve.wait_ge(s_egap, k + 1)
                chain.link(dve, dve.tensor_scalar(gate[:, 1, ts], egap[:, ts], 1.0, None, ALU.add))
                chain.link(dve, dve.reciprocal(gate[:, 0, ts], gate[:, 1, ts]))
                chain.link(dve, dve.tensor_tensor(gate[:, 1, ts], egap[:, ts], gate[:, 0, ts], ALU.mult))
                shape = [P, ts.stop - ts.start, E]

                def over(ap):
                    return ap.rearrange("q (t o) -> q t o", o=1).to_broadcast(shape)

                for r, c in ((0, comb), (1, comb2)):
                    chain.link(dve, dve.tensor_tensor(c[:, ts, :],
                                                      lane[:, :].rearrange("q (o e) -> q o e", o=1).to_broadcast(shape),
                                                      over(topf[:, ts, r]), ALU.is_equal))
                    chain.link(dve, dve.tensor_tensor(c[:, ts, :], c[:, ts, :], over(gate[:, r, ts]), ALU.mult))
                chain.link(dve, dve.tensor_tensor(comb[:, ts, :], comb[:, ts, :], comb2[:, ts, :], ALU.add))

            def split_first():
                for full, f, o, order in ((s_qf, qf[0], qs, (2, 1, 0)), (s_kf, kf[0], ks, (0, 1, 2))):
                    h, m, l = (o[:, a, :] for a in order)
                    dve.wait_ge(full, 1)
                    ins = dve.tensor_copy(h, f[:, :])
                    ins.then_inc(s_split, 1)
                    dve.wait_ge(s_split, 1 if o is qs else 4)
                    chain.link(dve, dve.tensor_tensor(f[:, :], f[:, :], h, ALU.subtract))
                    dve.tensor_copy(m, f[:, :]).then_inc(s_split, 1)
                    dve.wait_ge(s_split, 2 if o is qs else 5)
                    dve.tensor_tensor(l, f[:, :], m, ALU.subtract).then_inc(s_split, 1)

            def max_at(i, s):
                if s + LEAD < TILES:
                    row_max(i, s + LEAD)
                elif early(i, 7):
                    row_max(i + 1, s + LEAD - TILES)

            def head():
                dve.memset(qst[1][:, :, :, :], 0.0).then_inc(s_zero, 1)
                dve.wait_ge(s_x, 16)
                moments(0, 0, s_mv1)
                dve.memset(onesf[:, :], 1.0).then_inc(s_ones, 1)
                dve.memset(qst[0][ROWS:P, :, :, :], 0.0)
                dve.memset(vx[0][:, :, :, :, :], 1.0)
                split_first()
                dve.memset(vx[1][:, :, :, :, :], 1.0).then_inc(s_zero, 1)
                dve.wait_ge(s_x, 32)
                moments(0, 1, s_mv1)
                mask_flag(0)
                mask_flag(1)
                dve.wait_ge(s_ones, 1)
                dve.wait_ge(s_vo, 16 * 5)
                dve.tensor_scalar(bvb[:, :], onesf[:, :], bv_sb[:, 0:1], None, ALU.mult).then_inc(s_bvb, 1)
                moments(0, 2, s_mv1)
                dve.wait_ge(s_obp, 1)
                dve.tensor_tensor(obias[:, :], ps_a[:, 0:D], bo_sb[:, :], ALU.add).then_inc(s_ob, 1)
                for s in range(LEAD):
                    row_max(0, s)
                dve.wait_ge(s_resx, 1)

            def body(i, par):
                for s in range(CH):
                    max_at(i, s)
                    if s == DVE["flag"] and early(i, 6):
                        mask_flag(i + 2)
                    if s == DVE["normalise1"] and later(i):
                        normalise(i - 1, 1)
                    if s == DVE["residual"] and later(i):
                        residual(i - 1)
                    if s in DVE["moments2"] and later(i):
                        norm2_moments(i - 1, at(DVE["moments2"], s))
                    if s in DVE["moments1"] and early(i, 5):
                        moments(0, i + 3, s_mv1, at(DVE["moments1"], s))
                    if s == DVE["logits"] and later(i):
                        logits_copy(i - 1)
                    if s == 20 and not early(i, 7):
                        route_top(0)
                    if s == DVE["normalise0"]:
                        normalise(i, 0)
                    if s == 24 and not early(i, 7):
                        route(0)

            batches(dve, head, body, chain, 2 * (1 + 2 + 2 + 1))
            def gated(tc, u, first):
                e, f = u // FT, u % FT
                dve.wait_ge(s_act, 2 * E * tc + u + 1)
                dve.wait_ge(s_u, 2 * E * tc + u + 1)
                if not first:
                    dve.wait_ge(s_eo, E * tc + e - 1)
                dve.tensor_tensor(hid[e % 2][f][:, :], (ps_t, ps_s)[u % 2][1][:, :], act_sb[u % 2][:, :],
                                  ALU.mult).then_inc(s_hid, 1)

            def last_tail(e):
                if e == 0:
                    normalise(B - 1, 1)
                elif e == 2:
                    residual(B - 1)
                    norm2_moments(B - 1, range(3))
                elif e == 5:
                    logits_copy(B - 1)
                    route_top(1)

            def weigh(tc, e, first):
                dve.wait_ge(s_eo, E * tc + e + 1)
                if not first:
                    dve.wait_ge(s_sum, E * tc + e - 1)
                c = comb[:, bass.ts(tc, TT), e:e + 1].to_broadcast([P, TT, D])
                dve.tensor_tensor(part[e % 2][:, :].rearrange("q (t d) -> q t d", t=TT), (ps_b, ps_pv)[e % 2][:, :].rearrange("q (t d) -> q t d", t=TT), c,
                                  ALU.mult).then_inc(s_part, 1)

            def chunk_of_tokens(tc, first):
                for e in range(E):
                    for f in range(FT):
                        gated(tc, FT * e + f, first and e < 2)
                    if first and e:
                        last_tail(e - 1)
                    if e:
                        weigh(tc, e - 1, first and e - 1 < 2)
                weigh(tc, E - 1, False)
                if first:
                    route(1)

            chunk_of_tokens(0, True)
            with dve.Fori(1, TC) as tc:
                chunk_of_tokens(tc, False)


def kernel(x, ctx_1024, mask_BxSxS2_bf1, L0_xattn_Wq, L0_xattn_bq, L0_xattn_Wk, L0_xattn_bk, L0_xattn_Wv, L0_xattn_bv,
           L0_xattn_Wo, L0_xattn_bo, L0_ffn_router_w, L0_ffn_w1, L0_ffn_w3, L0_ffn_w2):
    import numpy as np
    import concourse.bacc as bacc
    from concourse.bass_utils import run_bass_kernel_spmd

    def turned(w):
        return np.ascontiguousarray(np.asarray(w).T)

    d = L0_xattn_Wv.shape[0]

    def regrouped(a, order):
        a = np.asarray(a)
        lead = a.shape[:-1]
        axes = tuple(range(len(lead))) + tuple(len(lead) + o for o in order)
        return np.ascontiguousarray(a.reshape(*lead, 2, 8, 8).transpose(axes).reshape(*lead, d))

    def by_two(w):
        return w.reshape(4, 2, *w.shape[1:]).transpose(0, 2, 1, 3).reshape(4, w.shape[1], -1)

    arrays = {
        "x": np.ascontiguousarray(x),
        "ctx_t": np.ascontiguousarray(np.asarray(ctx_1024).transpose(0, 2, 1)),
        "mask": np.ascontiguousarray(mask_BxSxS2_bf1).view(np.uint8),
        "wq_t": regrouped(turned(L0_xattn_Wq), (0, 2, 1)), "bq": regrouped(L0_xattn_bq, (0, 2, 1)),
        "wk_t": regrouped(turned(L0_xattn_Wk), (0, 2, 1)), "bk": regrouped(L0_xattn_bk, (0, 2, 1)),
        "wv_t": regrouped(turned(L0_xattn_Wv), (1, 0, 2)),
        "bv": np.ascontiguousarray(L0_xattn_bv),
        "wo_t": turned(L0_xattn_Wo), "bo": np.ascontiguousarray(L0_xattn_bo),
        "router_w": np.ascontiguousarray(L0_ffn_router_w),
        "w13": np.ascontiguousarray(np.concatenate([by_two(np.asarray(L0_ffn_w1)), by_two(np.asarray(L0_ffn_w3))])),
        "w2": np.ascontiguousarray(L0_ffn_w2),
    }
    nc = bacc.Bacc("TRN2", target_bir_lowering=False, num_devices=1)
    ins = {n: nc.dram_tensor(f"in_{n}", a.shape, mybir.dt.from_np(a.dtype), kind="ExternalInput").ap()
           for n, a in arrays.items()}
    out = nc.dram_tensor("out_x", arrays["x"].shape, F32, kind="ExternalOutput").ap()
    xattn_ffn_kernel(nc, **ins, out=out)
    r = run_bass_kernel_spmd(nc, [{f"in_{n}": a for n, a in arrays.items()}], core_ids=[0])
    return r.results[0]["out_x"]
```
